# Optimizing a Trainium2 kernel written in Bass

```python
import numpy as np
import jax
import jax.numpy as jnp

def _softmax(x, axis=-1):
    return jax.nn.softmax(x, axis=axis)

def _gelu(x):
    return jax.nn.gelu(x, approximate=True)

def _silu(x):
    return jax.nn.silu(x)

def _sigmoid(x):
    return jax.nn.sigmoid(x)

def _layernorm(x, axis=-1, eps=1e-05):
    m = jnp.mean(x, axis=axis, keepdims=True)
    v = jnp.var(x, axis=axis, keepdims=True)
    return (x - m) / jnp.sqrt(v + eps)

def _scatter_add(tgt, idx, src, axis=0):
    return tgt.at[idx].add(src)

def _segment_sum(src, seg, n):
    return jax.ops.segment_sum(src, seg, n)
kernel_name = 'mk_xattn_ffn_d1_seqx_r8_f24907'

def setup_inputs(seed: int=0):
    np.random.seed(seed)
    _w = jnp.asarray

    def _rec_inputs():
        import jax
        import jax.numpy as jnp
        _rk = jax.random.key(seed)
        x = -0.0002928 + 1 * jax.random.normal(jax.random.fold_in(_rk, 1), (32, 64, 128), jnp.float32)
        _lenS = 64 - jax.random.randint(jax.random.fold_in(_rk, 7), (32,), 0, max(1, 64 // 4) + 1, jnp.int32)
        _lenS2 = 64 - jax.random.randint(jax.random.fold_in(_rk, 8), (32,), 0, max(1, 64 // 4) + 1, jnp.int32)
        _ctx_1024P = jax.random.normal(jax.random.fold_in(_rk, 11), (32, 16, 128), jnp.float32)
        _ctx_1024c = jax.random.dirichlet(jax.random.fold_in(_rk, 511), 0.3 * jnp.ones((16,), jnp.float32), (32, 64))
        _ctx_1024t = jnp.einsum('bsk,bkd->bsd', _ctx_1024c, _ctx_1024P)
        _ctx_1024t = _ctx_1024t * jax.lax.rsqrt(jnp.mean(jnp.square(_ctx_1024t)) + 1e-12) * 0.953939
        ctx_1024 = -1.39393e-06 + 0.999914 * (_ctx_1024t + 0.3 * jax.random.normal(jax.random.fold_in(_rk, 611), (32, 64, 128), jnp.float32))
        return (x, ctx_1024)
    x, ctx_1024 = _rec_inputs()

    def _L0_xattn_setup():
        import jax, jax.numpy as jnp
        import numpy as np
        SCALE_BASE = 512.0
        GN_EPS = 1e-05

        def _xpos(x, downscale):
            L, D = (x.shape[-2], x.shape[-1])
            half = D // 2
            base = (jnp.arange(0, D, 2, dtype=jnp.float32) + 0.4 * D) / (1.4 * D)
            min_pos = -(L // 2)
            power = (jnp.arange(min_pos, min_pos + L, dtype=jnp.float32) / SCALE_BASE)[:, None]
            scale = base[None, :] ** power
            inv_freq = 1.0 / 10000.0 ** (jnp.arange(half, dtype=jnp.float32) / half)
            ang = jnp.arange(L, dtype=jnp.float32)[:, None] * inv_freq[None, :]
            sin, cos = (jnp.sin(ang), jnp.cos(ang))
            if downscale:
                scale = 1.0 / scale
            sin_s = jnp.repeat(sin * scale, 2, axis=-1)
            cos_s = jnp.repeat(cos * scale, 2, axis=-1)
            x1, x2 = (x[..., ::2], x[..., 1::2])
            rot = jnp.stack((-x2, x1), axis=-1).reshape(x.shape)
            return x * cos_s + rot * sin_s

        def _decay_mask(L, H):
            gammas = 1.0 - jnp.exp(jnp.linspace(np.log(1.0 / 32.0), np.log(1.0 / 512.0), H)).astype(jnp.float32)
            idx = jnp.arange(L)
            dist = idx[:, None] - idx[None, :]
            causal = dist >= 0
            d = jnp.maximum(dist, 0).astype(jnp.float32)
            return jnp.where(causal[None], gammas[:, None, None] ** d[None], 0.0)
        key = jax.random.key(seed)
        ks = jax.random.split(key, 9)
        B, L, D, H = (2, 256, 128, 16)
        hd = D // H
        return {'query': jax.random.normal(ks[0], (B, L, D), jnp.float32), 'key': jax.random.normal(ks[1], (B, L, D), jnp.float32), 'value': jax.random.normal(ks[2], (B, L, D), jnp.float32), 'W_Q': jax.random.normal(ks[3], (H, D, hd), jnp.float32) / D, 'W_K': jax.random.normal(ks[4], (H, D, hd), jnp.float32) / D, 'W_V': jax.random.normal(ks[5], (H, D, hd), jnp.float32) / D, 'g_w': jax.random.normal(ks[6], (D, D), jnp.float32) * (2.0 / (D + D)) ** 0.5, 'g_b': jnp.zeros((D,), jnp.float32), 'out_w': jax.random.normal(ks[7], (D, D), jnp.float32) * (2.0 / (D + D)) ** 0.5, 'out_b': jnp.zeros((D,), jnp.float32)}
    _L0_xattn_all = _L0_xattn_setup()
    _L0_xattn_in = {k: v for k, v in _L0_xattn_all.items() if k in ('W_Q', 'W_K', 'W_V', 'g_w', 'g_b', 'out_w', 'out_b')}
    del _L0_xattn_all

    def _L0_ffn_setup():
        import jax, jax.numpy as jnp
        import numpy as np
        D_MODEL = 128
        D_HIDDEN = 512
        NUM_EXPERTS = 8
        B, T = (2, 256)
        key = jax.random.key(seed)
        ks = jax.random.split(key, 8)
        s = 0.02
        x = jax.random.normal(ks[0], (B, T, D_MODEL), dtype=jnp.float32)
        Wg = jax.random.normal(ks[1], (D_MODEL, NUM_EXPERTS), dtype=jnp.float32) * s
        bg = jnp.zeros((NUM_EXPERTS,), dtype=jnp.float32)
        W1 = jax.random.normal(ks[2], (NUM_EXPERTS, D_MODEL, D_HIDDEN), dtype=jnp.float32) * s
        b1 = jnp.zeros((NUM_EXPERTS, D_HIDDEN), dtype=jnp.float32)
        W2 = jax.random.normal(ks[3], (NUM_EXPERTS, D_HIDDEN, D_MODEL), dtype=jnp.float32) * s
        b2 = jnp.zeros((NUM_EXPERTS, D_MODEL), dtype=jnp.float32)
        return {'x': x, 'Wg': Wg, 'bg': bg, 'W1': W1, 'b1': b1, 'W2': W2, 'b2': b2}
    _L0_ffn_all = _L0_ffn_setup()
    _L0_ffn_in = {k: v for k, v in _L0_ffn_all.items() if k in ('Wg', 'bg', 'W1', 'b1', 'W2', 'b2')}
    del _L0_ffn_all
    return {'x': x, 'ctx_1024': ctx_1024, 'L0_xattn_W_Q': _L0_xattn_in['W_Q'], 'L0_xattn_W_K': _L0_xattn_in['W_K'], 'L0_xattn_W_V': _L0_xattn_in['W_V'], 'L0_xattn_g_w': _L0_xattn_in['g_w'], 'L0_xattn_g_b': _L0_xattn_in['g_b'], 'L0_xattn_out_w': _L0_xattn_in['out_w'], 'L0_xattn_out_b': _L0_xattn_in['out_b'], 'L0_ffn_Wg': _L0_ffn_in['Wg'], 'L0_ffn_bg': _L0_ffn_in['bg'], 'L0_ffn_W1': _L0_ffn_in['W1'], 'L0_ffn_b1': _L0_ffn_in['b1'], 'L0_ffn_W2': _L0_ffn_in['W2'], 'L0_ffn_b2': _L0_ffn_in['b2']}

def reference(x, ctx_1024, L0_xattn_W_Q, L0_xattn_W_K, L0_xattn_W_V, L0_xattn_g_w, L0_xattn_g_b, L0_xattn_out_w, L0_xattn_out_b, L0_ffn_Wg, L0_ffn_bg, L0_ffn_W1, L0_ffn_b1, L0_ffn_W2, L0_ffn_b2):
    import jax
    import jax.numpy as jnp

    def _L0_xattn_ref(query, key, value, W_Q, W_K, W_V, g_w, g_b, out_w, out_b):
        import jax, jax.numpy as jnp
        import numpy as np
        SCALE_BASE = 512.0
        GN_EPS = 1e-05

        def _xpos(x, downscale):
            L, D = (x.shape[-2], x.shape[-1])
            half = D // 2
            base = (jnp.arange(0, D, 2, dtype=jnp.float32) + 0.4 * D) / (1.4 * D)
            min_pos = -(L // 2)
            power = (jnp.arange(min_pos, min_pos + L, dtype=jnp.float32) / SCALE_BASE)[:, None]
            scale = base[None, :] ** power
            inv_freq = 1.0 / 10000.0 ** (jnp.arange(half, dtype=jnp.float32) / half)
            ang = jnp.arange(L, dtype=jnp.float32)[:, None] * inv_freq[None, :]
            sin, cos = (jnp.sin(ang), jnp.cos(ang))
            if downscale:
                scale = 1.0 / scale
            sin_s = jnp.repeat(sin * scale, 2, axis=-1)
            cos_s = jnp.repeat(cos * scale, 2, axis=-1)
            x1, x2 = (x[..., ::2], x[..., 1::2])
            rot = jnp.stack((-x2, x1), axis=-1).reshape(x.shape)
            return x * cos_s + rot * sin_s

        def _decay_mask(L, H):
            gammas = 1.0 - jnp.exp(jnp.linspace(np.log(1.0 / 32.0), np.log(1.0 / 512.0), H)).astype(jnp.float32)
            idx = jnp.arange(L)
            dist = idx[:, None] - idx[None, :]
            causal = dist >= 0
            d = jnp.maximum(dist, 0).astype(jnp.float32)
            return jnp.where(causal[None], gammas[:, None, None] ** d[None], 0.0)
        B, L, D = query.shape
        H = W_Q.shape[0]
        q = jnp.einsum('bld,hde->bhle', query, W_Q)
        k = jnp.einsum('bld,hde->bhle', key, W_K)
        v = jnp.einsum('bld,hde->bhle', value, W_V)
        q = _xpos(q, downscale=False)
        k = _xpos(k, downscale=True)
        sim = jnp.einsum('bhnd,bhsd->bhns', q, k) * _decay_mask(L, H)[None]
        ret = jnp.einsum('bhns,bhsd->bhnd', sim, v)
        mu = ret.mean(axis=-1, keepdims=True)
        var = ret.var(axis=-1, keepdims=True)
        ret = (ret - mu) / jnp.sqrt(var + GN_EPS)
        ret = ret.transpose(0, 2, 1, 3).reshape(B, L, D)
        gate = jax.nn.silu(query @ g_w.T + g_b)
        return ret * gate @ out_w.T + out_b

    def _L0_ffn_ref(x, Wg, bg, W1, b1, W2, b2):
        import jax, jax.numpy as jnp
        import numpy as np
        D_MODEL = 128
        D_HIDDEN = 512
        NUM_EXPERTS = 8
        B, T = (2, 256)
        gate_logits = jnp.einsum('btd,de->bte', x, Wg) + bg
        gate_scores = jax.nn.softmax(gate_logits, axis=-1)
        top1_idx = jnp.argmax(gate_scores, axis=-1)
        top1_mask = jax.nn.one_hot(top1_idx, NUM_EXPERTS, dtype=x.dtype)
        top1_weight = jnp.sum(gate_scores * top1_mask, axis=-1, keepdims=True)
        h = jax.nn.silu(jnp.einsum('btd,edh->bteh', x, W1) + b1)
        o = jnp.einsum('bteh,ehd->bted', h, W2) + b2
        y = jnp.sum(o * top1_mask[..., None], axis=2) * top1_weight
        return y
    x = x + _L0_xattn_ref(_layernorm(x, axis=-1), ctx_1024, ctx_1024, L0_xattn_W_Q, L0_xattn_W_K, L0_xattn_W_V, L0_xattn_g_w, L0_xattn_g_b, L0_xattn_out_w, L0_xattn_out_b)
    x = x + _L0_ffn_ref(_layernorm(x, axis=-1), L0_ffn_Wg, L0_ffn_bg, L0_ffn_W1, L0_ffn_b1, L0_ffn_W2, L0_ffn_b2)
    return x

_drawn_inputs = setup_inputs


def setup_inputs(seed=0):
    import zlib

    import numpy as np

    out = dict(_drawn_inputs(seed))
    spreads = {'L0_xattn_g_b': (0.0, 0.1),
     'L0_xattn_out_b': (0.0, 0.1),
     'L0_ffn_bg': (0.0, 0.73),
     'L0_ffn_b1': (0.0, 0.8),
     'L0_ffn_b2': (0.0, 0.524)}
    factors = {'L0_ffn_Wg': 3.51, 'L0_ffn_W1': 7.03, 'L0_ffn_W2': 6.433}
    for name, (base, spread) in spreads.items():
        noise = np.random.default_rng([zlib.crc32(name.encode()), seed]).standard_normal(out[name].shape)
        drawn = base * np.exp(spread * noise) if base else spread * noise
        out[name] = jnp.asarray(drawn.astype(out[name].dtype))
    for name, factor in factors.items():
        out[name] = (out[name] * factor).astype(out[name].dtype)
    return out
```

```python
from contextlib import ExitStack

import numpy as np
import concourse.bass as bass
from concourse import mybir

F32 = mybir.dt.float32
BF16 = mybir.dt.bfloat16
I32 = mybir.dt.int32
ALU = mybir.AluOpType
ACT = mybir.ActivationFunctionType
AX = mybir.AxisListType

P = 128
BATCH, SEQ, D = 32, 64, 128
HEADS, HD = 16, 8
TOKENS = BATCH * SEQ
TILES = TOKENS // P
UNIT = 2 * P
UNITS = TOKENS // UNIT
UB = UNIT // SEQ
GROUPS = 4
GH = HEADS // GROUPS
Q = 32
QUARTER = TOKENS // 4
QT = TILES // 4
EXPERTS, HIDDEN = 8, 512
HC = HIDDEN // P
SLOT_TILES = TILES + EXPERTS - 1
ROW = 2 * D + 1
EPS = 1e-5
RING = 12
NO_TOKEN = 1 << 16

CONST_PARTS = [("ident", P), ("rotary", 4 * SEQ), ("causal", SEQ), ("head_in_group", GH),
               ("centre", P), ("head_mean", Q), ("spread", 4 * P), ("before", P), ("ones", P),
               ("iota", P), ("tile_no", TILES), ("expert_rank", EXPERTS), ("tile_edge", TILES),
               ("not_first_tile", EXPERTS * TILES), ("partition", 1)]
CONST_AT, _at = {}, 0
for _name, _width in CONST_PARTS:
    CONST_AT[_name] = (_at, _width)
    _at += _width
CONST_WIDTH = _at
EARLY_CONSTS = CONST_AT["head_mean"][0]
ATTN_WEIGHTS = ["q", "q_pair_swapped", "k", "k_pair_swapped", "v_transposed", "gate", "out"]


def build(nc, x, ctx, w_attn, g_b, out_b, w_gate, b_gate, w1, b1, w2, b2, consts, out):
    stack = ExitStack()
    with stack:
        def sb(name, shape, dt=F32):
            return stack.enter_context(nc.sbuf_tensor(name, shape, dt))

        def bank(name):
            return stack.enter_context(nc.psum_tensor(name, [P, 512], F32))

        def sem(name):
            return stack.enter_context(nc.semaphore(name))

        token_rows = nc.dram_tensor("token_rows", [TOKENS, ROW], F32, kind="Internal").ap()

        cst = sb("cst", [P, CONST_WIDTH])
        wat = sb("wat", [P, len(ATTN_WEIGHTS), P])
        w_v = sb("w_v", [P, P])
        warm = sb("warm", [P, 512], BF16)
        unused = sb("unused", [P, 4])
        gate_bias = sb("gate_bias", [P, 1])
        out_bias = sb("out_bias", [P, D])
        router_bias = sb("router_bias", [P, EXPERTS])
        router_w = sb("router_w", [P, Q])
        w1_all = sb("w1_all", [P, EXPERTS * HIDDEN])
        w2_all = sb("w2_all", [P, EXPERTS * HC * D])
        b1_all = sb("b1_all", [P, EXPERTS * HC])
        b2_all = sb("b2_all", [P, EXPERTS * D])
        x_all = sb("x_all", [P, TILES, D])
        x_plus_b = sb("x_plus_b", [P, TILES, D])
        stats = sb("stats", [P, TILES, 6])
        mean_var = sb("mean_var", [P, TILES, 2])
        std = sb("std", [P, TILES])
        rstd = sb("rstd", [P, TILES])
        xn = [sb(f"xn{r}", [P, 2, D]) for r in range(2)]
        ctx_in = [sb(f"ctx_in{r}", [P, 2, D]) for r in range(2)]
        xcT = [sb(f"xcT{r}", [P, 2 * UNIT]) for r in range(2)]
        q_parts = sb("q_parts", [P, 2, UNIT])
        k_parts = sb("k_parts", [P, 2, UNIT])
        q_sum = [sb(f"q_sum{r}", [P, UNIT]) for r in range(2)]
        k_sum = [sb(f"k_sum{r}", [P, UNIT]) for r in range(2)]
        q_heads = [sb(f"q_heads{r}", [P, UB, GH, SEQ]) for r in range(2)]
        k_groups = [sb(f"k_groups{r}", [P, GROUPS, UNIT]) for r in range(2)]
        v_batches = [sb(f"v_batches{r}", [P, 2, 2, P]) for r in range(2)]
        sim = [sb(f"sim{j}", [P, 2, 512]) for j in range(2)]
        ret_sum = [sb(f"ret_sum{j}", [P, GH - 1, P]) for j in range(2)]
        retT = sb("retT", [P, TOKENS])
        gateT = sb("gateT", [P, TOKENS])
        ret_gate = sb("ret_gate", [P, TOKENS])
        squares = x_all[:, :, :].rearrange("p t d -> p (t d)")
        head_var = sb("head_var", [P, 512])
        head_std = sb("head_std", [P, 512])
        head_rstd = sb("head_rstd", [P, 512])
        attn = [sb(f"attn{r}", [P, QUARTER]) for r in range(2)]
        rows = sb("rows", [P, TILES, 2 * D])
        stats2 = sb("stats2", [P, TILES, 6])
        mean_var2 = sb("mean_var2", [P, TILES, 2])
        var_eps2 = sb("var_eps2", [P, TILES])
        std2 = sb("std2", [P, TILES])
        rstd2 = sb("rstd2", [P, TILES])
        xn2T = retT
        logitsT = sb("logitsT", [P, 512])
        te = [P, TILES, EXPERTS]
        logits = sb("logits", te)
        top = sb("top", [P, TILES])
        below_top = sb("below_top", te)
        powers = sb("powers", te)
        power_sum = sb("power_sum", [P, TILES])
        top_weight = sb("top_weight", [P, TILES])
        is_top = sb("is_top", te)
        rank_of_top = sb("rank_of_top", te)
        best_rank = sb("best_rank", [P, TILES])
        chosen = sb("chosen", te)
        counts = sb("counts", [P, EXPERTS, TILES])
        counts_to = sb("counts_to", [P, EXPERTS, TILES])
        tiles_used = sb("tiles_used", [P, EXPERTS, TILES])
        n_tiles = sb("n_tiles", [P, EXPERTS])
        end_tile = sb("end_tile", [P, EXPERTS])
        base = sb("base", [P, EXPERTS])
        counts_before = sb("counts_before", [P, EXPERTS, TILES])
        place = sb("place", te)
        place_b = sb("place_b", te)
        place_chosen = sb("place_chosen", te)
        slot = sb("slot", [P, TILES])
        slot_i = sb("slot_i", [P, TILES], I32)
        slot_parts_i = sb("slot_parts_i", [P, 2, TILES], I32)
        slot_parts = sb("slot_parts", [P, 2, TILES])
        past_end = sb("past_end", [P, SLOT_TILES, EXPERTS])
        tile_expert_f = sb("tile_expert_f", [P, SLOT_TILES])
        tile_expert = sb("tile_expert", [P, SLOT_TILES], I32)
        in_tile = sb("in_tile", [P, TILES, 3, SLOT_TILES], BF16)
        in_lane = sb("in_lane", [P, TILES, P], BF16)
        iota_b = sb("iota_b", [P, P], BF16)
        inverse = sb("inverse", [P, 3, SLOT_TILES])
        source = sb("source", [P, SLOT_TILES])
        target = sb("target", [P, SLOT_TILES])
        indices = sb("indices", [P, 2, SLOT_TILES], I32)
        got_rows = [sb(f"got_rows{u}", [P, ROW]) for u in range(RING)]
        slotT = [sb(f"slotT{r}", [P, P]) for r in range(2)]
        w1_now = [sb(f"w1_now{r}", [P, HIDDEN]) for r in range(2)]
        hiddenT = [sb(f"hiddenT{r}", [P, HC, P]) for r in range(2)]
        y_bias = [sb(f"y_bias{r}", [P, D]) for r in range(2)]

        bank_t, bank_q, bank_k, bank_gv = (bank(f"bank_{n}") for n in ("t", "q", "k", "gv"))
        bank_s = [bank(f"bank_s{i}") for i in range(2)]
        bank_o = [bank(f"bank_o{i}") for i in range(2)]

        def const(name, *dims):
            at, width = CONST_AT[name]
            part = cst[:, at:at + width]
            if dims:
                part = part.rearrange("p (a b) -> p a b", a=dims[0])
            return part

        consts_in, late_consts_in, attn_w_in, bias_in, expert_w_in = map(
            sem, ("consts_in", "late_consts_in", "attn_w_in", "bias_in", "expert_w_in"))
        x_in = [sem(f"x_in{c}") for c in range(4)]
        ctx_ld = [sem(f"ctx_ld{r}") for r in range(2)]
        zeroed, warm_zeroed = map(sem, ("zeroed", "warm_zeroed"))
        xb_done = sem("xb_done")
        dve_step = sem("dve_step")
        var_done, std_done, rstd_done = map(sem, ("var_done", "std_done", "rstd_done"))
        wv_done, wv_copied = map(sem, ("wv_done", "wv_copied"))
        xn_done, xT_done, xcT_done = map(sem, ("xn_done", "xT_done", "xcT_done"))
        q_done, k_done, gv_done = map(sem, ("q_done", "k_done", "gv_done"))
        q_rotated, k_rotated, q_summed, k_summed = map(sem, ("q_rotated", "k_rotated", "q_summed", "k_summed"))
        qh_done, kg_done, gv_copied = map(sem, ("qh_done", "kg_done", "gv_copied"))
        scores_done, sim_done, av_done = map(sem, ("scores_done", "sim_done", "av_done"))
        head0_done, head_added, ret_done = map(sem, ("head0_done", "head_added", "ret_done"))
        squared, ret_gated, hvar_done, hvar_eps, hstd_done, hrstd_done = map(
            sem, ("squared", "ret_gated", "hvar_done", "hvar_eps", "hstd_done", "hrstd_done"))
        spread_done, attn_done, proj_done, x1_done = map(sem, ("spread_done", "attn_done", "proj_done", "x1_done"))
        var2_done, std2_done, xn2_done, xn2T_done, xn2T_copied = map(
            sem, ("var2_done", "std2_done", "xn2_done", "xn2T_done", "xn2T_copied"))
        logitsT_done, logitsT_copied, logits_turned = map(sem, ("logitsT_done", "logitsT_copied", "logits_turned"))
        below_done, powers_done, weight_done = map(sem, ("below_done", "powers_done", "weight_done"))
        chosen_done, ranks_done, lanes_done, inverse_done, indices_done = map(
            sem, ("chosen_done", "ranks_done", "lanes_done", "inverse_done", "indices_done"))
        rows_out, weights_out = map(sem, ("rows_out", "weights_out"))
        got = [sem(f"got{u}") for u in range(RING)]
        scattered = [sem(f"scattered{u}") for u in range(RING)]
        slotT_done, slotT_copied, w1_copied = map(sem, ("slotT_done", "slotT_copied", "w1_copied"))
        hidden_done, silu_done, y_done, y_biased, out_done = map(
            sem, ("hidden_done", "silu_done", "y_done", "y_biased", "out_done"))

        START = 4 + 1
        ring_counts = [xT_done, gv_done, scores_done, av_done, ret_done, sim_done, kg_done, qh_done,
                       slotT_copied, hidden_done, silu_done, y_done, y_biased]

        block = stack.enter_context(nc.Block())

        @block.sync
        def _(sp):
            x_tiles = x.rearrange("(t p) d -> p t d", p=P)
            ctx_units = ctx.rearrange("(m j p) d -> m p j d", p=P, j=2)

            def load_ctx(m, r):
                sp.wait_ge(xT_done, START + m - 1)
                sp.dma_start(ctx_in[r][:, :, :],
                             ctx_units[m] if isinstance(m, int)
                             else ctx_units[bass.ds(m, 1)].rearrange("m p j d -> (m p) j d")
                             ).then_inc(ctx_ld[r], 16)

            for c in range(4):
                sp.dma_start(x_all[:, QT * c:QT * c + QT, :], x_tiles[:, QT * c:QT * c + QT, :]).then_inc(x_in[c], 16)
                if c == 0:
                    load_ctx(0, 0)
                    sp.dma_start(wat[:, :, :], w_attn).then_inc(attn_w_in, 16)
            load_ctx(1, 1)
            sp.dma_start(out_bias[:, :], out_b.partition_broadcast(P)).then_inc(bias_in, 16)
            sp.dma_start(router_bias[:, :], b_gate.partition_broadcast(P)).then_inc(bias_in, 16)
            sp.dma_start(router_w[:, :], w_gate).then_inc(bias_in, 16)
            sp.dma_start(cst[:, EARLY_CONSTS:CONST_WIDTH], consts[:, EARLY_CONSTS:CONST_WIDTH]).then_inc(late_consts_in, 16)
            for m in range(2, UNITS):
                load_ctx(m, m % 2)
            sp.dma_start(w1_all[:, :], w1).then_inc(expert_w_in, 16)
            sp.dma_start(w2_all[:, :], w2).then_inc(expert_w_in, 16)
            sp.dma_start(b1_all[:, :], b1).then_inc(expert_w_in, 16)
            sp.dma_start(b2_all[:, :], b2.partition_broadcast(P)).then_inc(expert_w_in, 16)
            row_tiles = token_rows.rearrange("(t p) r -> p t r", p=P)
            for c in range(4):
                sp.wait_ge(xn2_done, c + 1)
                sp.dma_start(row_tiles[:, QT * c:QT * c + QT, 0:2 * D], rows[:, QT * c:QT * c + QT, :]
                             ).then_inc(rows_out, 16)
            sp.wait_ge(weight_done, 1)
            with nc.allow_non_contiguous_dma(reason="one weight per token"):
                sp.dma_start(row_tiles[:, :, 2 * D:ROW], top_weight[:, :].unsqueeze(2)).then_inc(weights_out, 16)

        @block.gpsimd
        def _(pool):
            for count in ring_counts:
                pool.sem_inc(count, START)
            for r in range(2):
                pool.memset(k_groups[r][:, :, :], 0.0).then_inc(zeroed, 1)
                pool.memset(v_batches[r][:, :, :, :], 0.0).then_inc(zeroed, 1)

            def add_k(m, r):
                pool.wait_ge(k_rotated, m + 1)
                pool.wait_ge(kg_done, START + m - 1)
                pool.tensor_tensor(k_sum[r][:, :], k_parts[:, 0, :], k_parts[:, 1, :], ALU.add).then_inc(k_summed, 1)

            add_k(0, 0)
            pool.wait_ge(bias_in, 64)
            for c in range(4):
                pool.wait_ge(x_in[c], 16)
                tiles = slice(QT * c, QT * c + QT)
                pool.tensor_tensor(x_plus_b[:, tiles, :], x_all[:, tiles, :],
                                   out_bias[:, :].unsqueeze(1).broadcast_to([P, QT, D]), ALU.add).then_inc(xb_done, 1)
                if c == 0:
                    add_k(1, 1)
            with pool.Fori(0, (UNITS - 2) // 2) as n:
                for r in range(2):
                    add_k(2 * n + 2 + r, r)
            for c in range(4):
                cols = slice(QUARTER * c, QUARTER * c + QUARTER)
                pool.wait_ge(ret_done, START + QT * (c + 1))
                pool.wait_ge(gv_copied, 2 * (c + 1))
                pool.tensor_tensor(ret_gate[:, cols], retT[:, cols], gateT[:, cols], ALU.mult).then_inc(ret_gated, 1)

            last_row = pool.to_reg(TOKENS - 1)
            pool.wait_ge(indices_done, 1)
            pool.wait_ge(rows_out, 64)
            pool.wait_ge(weights_out, 16)


            def gather(i):
                u = i % RING
                if i >= RING:
                    pool.wait_ge(scattered[u], 16 * (i // RING))
                pool.indirect_dma_start(out=got_rows[u][:, :], out_offset=None, in_=token_rows[:, :],
                                        in_offset=bass.IndirectOffsetOnAxis(ap=indices[:, 0, i:i + 1], axis=0),
                                        bounds_check=last_row, oob_is_err=False).then_inc(got[u], 16)

            def scatter(i):
                pool.wait_ge(out_done, i + 1)
                pool.indirect_dma_start(out=out[:, :],
                                        out_offset=bass.IndirectOffsetOnAxis(ap=indices[:, 1, i:i + 1], axis=0),
                                        in_=got_rows[i % RING][:, 0:D], in_offset=None,
                                        bounds_check=last_row, oob_is_err=False).then_inc(scattered[i % RING], 16)

            AHEAD = RING - 2
            for i in range(AHEAD):
                gather(i)
            for i in range(SLOT_TILES):
                if i + AHEAD < SLOT_TILES:
                    gather(i + AHEAD)
                scatter(i)
            for u in range(RING):
                pool.wait_ge(scattered[u], 16 * len(range(u, SLOT_TILES, RING)))

        @block.scalar
        def _(act):
            act.dma_start(cst[:, 0:EARLY_CONSTS], consts[:, 0:EARLY_CONSTS]).then_inc(consts_in, 16)
            act.wait_ge(warm_zeroed, 1)
            nc.scalar.activation(unused[:, 0:1], warm[:, 0:1], ACT.Sqrt)
            act.dma_start(gate_bias[:, :], g_b).then_inc(bias_in, 16)
            def roots(tiles, step):
                act.wait_ge(var_done, step)
                nc.scalar.activation(std[:, tiles], rstd[:, tiles], ACT.Sqrt).then_inc(std_done, 1)

            roots(slice(0, QT), 1)
            act.wait_ge(wv_done, 1)
            nc.scalar.activation(w_v[:, :], bank_gv[:, 0:P], ACT.Copy).then_inc(wv_copied, 1)
            head_mask = const("head_in_group")

            def copy_transposed(m, r):
                act.wait_ge(xT_done, START + m + 1)
                act.wait_ge(gv_done, START + m - 1)
                nc.scalar.activation(xcT[r][:, :], bank_t[:, :], ACT.Copy).then_inc(xcT_done, 1)

            def split_q(m, r):
                act.wait_ge(q_summed, m + 1)
                act.wait_ge(scores_done, START + 4 * (m - 1))
                for h in range(GH):
                    last = nc.scalar.activation(q_heads[r][:, :, h, :], q_sum[r][:, :].rearrange("p (b i) -> p b i", b=UB),
                                                ACT.Copy, scale=head_mask[:, h:h + 1])
                last.then_inc(qh_done, 1)

            def split_k(m, r):
                act.wait_ge(k_summed, m + 1)
                act.wait_ge(scores_done, START + 4 * (m - 1))
                for g in range(GROUPS):
                    last = nc.scalar.activation(k_groups[r][Q * g:Q * g + Q, g, :], k_sum[r][Q * g:Q * g + Q, :], ACT.Copy)
                last.then_inc(kg_done, 1)

            def gate_and_values(m, r):
                act.wait_ge(gv_done, START + m + 1)
                act.wait_ge(av_done, START + 2 * (m - 1))
                nc.scalar.activation(gateT[:, bass.ds(m * UNIT, UNIT)], bank_gv[:, 0:UNIT], ACT.Silu,
                                     bias=gate_bias[:, 0:1])
                values = bank_gv[:, UNIT:2 * UNIT].rearrange("p (j f) -> p j f", j=2)
                nc.scalar.activation(v_batches[r][0:64, :, 0, :], values[0:64], ACT.Copy)
                nc.scalar.activation(v_batches[r][64:128, :, 1, :], values[64:128], ACT.Copy).then_inc(gv_copied, 1)

            def first_head(m, j):
                tile = 2 * m + j
                act.wait_ge(av_done, START + tile + 1)
                act.wait_ge(ret_done, START + tile)
                nc.scalar.activation(ret_sum[j][:, 0, :].rearrange("p (b i) -> p b i", b=2),
                                     bank_o[j][:, :].rearrange("p (b h i) -> p b h i", b=2, h=GH)[:, :, 0, :],
                                     ACT.Copy, scale=head_mask[:, 0:1]).then_inc(head0_done, 1)

            def unit(m, r, more=True):
                if more:
                    copy_transposed(m + 1, 1 - r)
                first_head(m, 0)
                if more:
                    split_q(m + 1, 1 - r)
                    split_k(m + 1, 1 - r)
                    gate_and_values(m + 1, 1 - r)
                first_head(m, 1)

            copy_transposed(0, 0)
            act.wait_ge(bias_in, 64)
            act.wait_ge(consts_in, 16)
            act.wait_ge(zeroed, 4)
            roots(slice(QT, TILES), 2)
            nc.scalar.activation(unused[:, 1:2], warm[:, 0:1], ACT.Silu)
            split_q(0, 0)
            gate_and_values(0, 0)
            with act.Fori(0, (UNITS - 2) // 2) as n:
                for r in range(2):
                    unit(2 * n + r, r)
            unit(UNITS - 2, 0)
            unit(UNITS - 1, 1, more=False)

            for c in range(4):
                cols = slice(QUARTER * c, QUARTER * c + QUARTER)
                act.wait_ge(ret_done, START + QT * (c + 1))
                act.wait_ge(xb_done, c + 1)
                nc.scalar.activation(squares[:, cols], retT[:, cols], ACT.Square).then_inc(squared, 1)
            act.wait_ge(hvar_eps, 1)
            nc.scalar.activation(head_std[:, :], head_var[:, :], ACT.Sqrt).then_inc(hstd_done, 1)

            def copy_xn2T(c):
                act.wait_ge(xn2T_done, c + 1)
                nc.scalar.activation(xn2T[:, QUARTER * c:QUARTER * c + QUARTER], bank_s[c % 2][:, :], ACT.Copy
                                     ).then_inc(xn2T_copied, 1)

            for c in range(4):
                act.wait_ge(var2_done, c + 1)
                nc.scalar.activation(std2[:, QT * c:QT * c + QT], var_eps2[:, QT * c:QT * c + QT], ACT.Sqrt
                                     ).then_inc(std2_done, 1)
                if c >= 1:
                    copy_xn2T(c - 1)
            copy_xn2T(3)
            act.wait_ge(below_done, 1)
            nc.scalar.activation(powers[:, :, :], below_top[:, :, :], ACT.Exp).then_inc(powers_done, 1)

            act.wait_ge(expert_w_in, 64)
            act.wait_ge(indices_done, 1)

            def silu(i, r):
                e = act.value_load(tile_expert[0:1, bass.ds(i, 1)], min_val=0, max_val=EXPERTS - 1)
                act.wait_ge(hidden_done, START + i + 1)
                act.wait_ge(y_done, START + i - 1)
                h_bank = (bank_q, bank_k)[r]
                for c in range(HC):
                    last = nc.scalar.activation(hiddenT[r][:, c, :], h_bank[:, P * c:P * c + P], ACT.Silu,
                                                bias=b1_all[:, bass.ds(e * HC + c, 1)])
                last.then_inc(silu_done, 1)

            for i in range(SLOT_TILES):
                silu(i, i % 2)

        @block.vector
        def _(dve):
            steps = [0]

            def chain(ins):
                steps[0] += 1
                ins.then_inc(dve_step, 1)
                dve.wait_ge(dve_step, steps[0])

            nc.vector.memset(warm[:, :], 0.0).then_inc(warm_zeroed, 1)

            def statistics(first, end):
                for t in range(first, end):
                    if t % QT == 0:
                        dve.wait_ge(x_in[t // QT], 16)
                    last = nc.vector.bn_stats(stats[:, t, :], x_all[:, t, :])
                return last

            def variances(first, end):
                for t in range(first, end):
                    last = nc.vector.bn_aggr(mean_var[:, t, :], stats[:, t, :])
                chain(last)
                nc.vector.tensor_scalar(rstd[:, first:end], mean_var[:, first:end, 1], EPS, None, ALU.add
                                        ).then_inc(var_done, 1)

            def invert_std(first, end, step):
                dve.wait_ge(std_done, step)
                nc.vector.reciprocal(rstd[:, first:end], std[:, first:end]).then_inc(rstd_done, 1)
                dve.wait_ge(rstd_done, step)

            chain(statistics(0, QT))
            variances(0, QT)
            invert_std(0, QT, 1)

            rotary = const("rotary", 4)
            causal = const("causal").unsqueeze(1).broadcast_to([P, 2 * GH, SEQ])
            head_mask = const("head_in_group")

            def normalise(m, r):
                dve.wait_ge(xT_done, START + m - 1)
                for j in range(2):
                    tile = 2 * m + j
                    last = nc.vector.tensor_scalar(
                        xn[r][:, j, :], x_all[:, bass.ds(tile, 1), :].rearrange("p a d -> p (a d)"),
                        mean_var[:, bass.ds(tile, 1), 0:1].rearrange("p a b -> p (a b)"),
                        rstd[:, bass.ds(tile, 1)], ALU.subtract, ALU.mult)
                last.then_inc(xn_done, 1)

            def rotate(parts, bank, table):
                return nc.vector.tensor_tensor(
                    parts[:, :, :].rearrange("p s (b i) -> p s b i", b=UB),
                    bank[:, :].rearrange("p (s b i) -> p s b i", s=2, b=UB),
                    rotary[:, table:table + 2, :].unsqueeze(2).broadcast_to([P, 2, UB, SEQ]), ALU.mult)

            def rotate_qk(m, r):
                dve.wait_ge(q_done, m + 1)
                dve.wait_ge(q_summed, m)
                rotate(q_parts, bank_q, 0).then_inc(q_rotated, 1)
                dve.wait_ge(k_done, m + 1)
                dve.wait_ge(k_summed, m)
                rotate(k_parts, bank_k, 2).then_inc(k_rotated, 1)
                dve.wait_ge(q_rotated, m + 1)
                dve.wait_ge(qh_done, START + m - 1)
                nc.vector.tensor_tensor(q_sum[r][:, :], q_parts[:, 0, :], q_parts[:, 1, :], ALU.add
                                        ).then_inc(q_summed, 1)

            def mask_scores(m, j):
                tile = 2 * m + j
                for gp in range(2):
                    dve.wait_ge(scores_done, START + 4 * m + 2 * j + gp + 1)
                    if gp == 0:
                        dve.wait_ge(av_done, START + tile)
                    nc.vector.tensor_tensor(sim[j][:, gp, :].rearrange("p (h i) -> p h i", i=SEQ),
                                            bank_s[gp][:, :].rearrange("p (h i) -> p h i", i=SEQ),
                                            causal, ALU.mult).then_inc(sim_done, 1)

            def add_heads(m, j):
                tile = 2 * m + j
                products = bank_o[j][:, :].rearrange("p (b h i) -> p b h i", b=2, h=GH)
                dve.wait_ge(head0_done, tile + 1)
                for h in range(1, GH):
                    if h > 1:
                        dve.wait_ge(head_added, 2 * tile + h - 1)
                    before = ret_sum[j][:, h - 1, :].rearrange("p (b i) -> p b i", b=2)
                    after = ret_sum[j][:, h, :] if h < GH - 1 else retT[:, bass.ds(tile * P, P)]
                    ins = nc.vector.scalar_tensor_tensor(
                        out=after.rearrange("p (b i) -> p b i", b=2), in0=products[:, :, h, :],
                        scalar=head_mask[:, h:h + 1], in1=before, op0=ALU.mult, op1=ALU.add)
                    ins.then_inc(head_added if h < GH - 1 else ret_done, 1)

            def unit(m, r, more=1):
                mask_scores(m, 0)
                if more:
                    rotate_qk(m + 1, 1 - r)
                add_heads(m, 0)
                mask_scores(m, 1)
                if more == 2 or more is True:
                    normalise(m + 2, r)
                add_heads(m, 1)

            normalise(0, 0)
            normalise(1, 1)
            chain(statistics(QT, TILES))
            variances(QT, TILES)
            dve.wait_ge(consts_in, 16)
            rotate_qk(0, 0)
            invert_std(QT, TILES, 2)
            dve.wait_ge(k_summed, 1)
            dve.wait_ge(zeroed, 4)
            for g in range(GROUPS):
                last = nc.vector.tensor_copy(k_groups[0][Q * g:Q * g + Q, g, :], k_sum[0][Q * g:Q * g + Q, :])
            last.then_inc(kg_done, 1)
            with dve.Fori(0, (UNITS - 2) // 2) as n:
                for r in range(2):
                    unit(2 * n + r, r, more=2)
            unit(UNITS - 2, 0, more=1)
            unit(UNITS - 1, 1, more=0)

            dve.wait_ge(hvar_done, 1)
            nc.vector.tensor_scalar(head_var[:, :], bank_t[:, :], EPS, None, ALU.add).then_inc(hvar_eps, 1)
            dve.wait_ge(hstd_done, 1)
            nc.vector.reciprocal(head_rstd[:, :], head_std[:, :]).then_inc(hrstd_done, 1)

            def close_attention(c):
                dve.wait_ge(spread_done, c + 1)
                dve.wait_ge(ret_gated, c + 1)
                if c >= 2:
                    dve.wait_ge(proj_done, c - 1)
                nc.vector.tensor_tensor(attn[c % 2][:, :], (bank_q, bank_k)[c % 2][:, :],
                                        ret_gate[:, QUARTER * c:QUARTER * c + QUARTER], ALU.mult
                                        ).then_inc(attn_done, 1)

            def residual(c):
                tiles = slice(QT * c, QT * c + QT)
                dve.wait_ge(proj_done, c + 1)
                dve.wait_ge(xb_done, c + 1)
                nc.vector.tensor_tensor(rows[:, tiles, D:2 * D],
                                        bank_o[c % 2][:, :].rearrange("p (t d) -> p t d", d=D),
                                        x_plus_b[:, tiles, :], ALU.add).then_inc(x1_done, 1)
                dve.wait_ge(x1_done, c + 1)
                for t in range(QT * c, QT * c + QT):
                    last = nc.vector.bn_stats(stats2[:, t, :], rows[:, t, D:2 * D])
                chain(last)
                for t in range(QT * c, QT * c + QT):
                    last = nc.vector.bn_aggr(mean_var2[:, t, :], stats2[:, t, :])
                chain(last)
                nc.vector.tensor_scalar(var_eps2[:, tiles], mean_var2[:, tiles, 1], EPS, None, ALU.add
                                        ).then_inc(var2_done, 1)

            def normalise2(c):
                tiles = slice(QT * c, QT * c + QT)
                dve.wait_ge(std2_done, c + 1)
                chain(nc.vector.reciprocal(rstd2[:, tiles], std2[:, tiles]))
                for t in range(QT * c, QT * c + QT):
                    last = nc.vector.tensor_scalar(rows[:, t, 0:D], rows[:, t, D:2 * D], mean_var2[:, t, 0:1],
                                                   rstd2[:, t:t + 1], ALU.subtract, ALU.mult)
                last.then_inc(xn2_done, 1)

            close_attention(0)
            close_attention(1)
            for c in range(4):
                residual(c)
                if c + 2 < 4:
                    close_attention(c + 2)
                if c >= 1:
                    normalise2(c - 1)
            normalise2(3)
            dve.wait_ge(late_consts_in, 16)
            nc.vector.tensor_copy(iota_b[:, :], const("iota"))

            dve.wait_ge(logitsT_done, 1)
            nc.vector.tensor_copy(logitsT[:, :], bank_gv[:, :]).then_inc(logitsT_copied, 1)
            dve.wait_ge(logits_turned, 1)
            turned = bank_t[:, :].rearrange("p (k c e) -> p c k e", k=QT, c=4)[:, :, :, 0:EXPERTS]
            chain(nc.vector.tensor_tensor(
                logits[:, :, :].rearrange("p (c k) e -> p c k e", c=4), turned,
                router_bias[:, :].unsqueeze(1).unsqueeze(1).broadcast_to([P, 4, QT, EXPERTS]), ALU.add))
            chain(nc.vector.tensor_reduce(top[:, :], logits[:, :, :], AX.X, ALU.max))
            top_b = top[:, :].unsqueeze(2).broadcast_to(te)
            nc.vector.tensor_tensor(below_top[:, :, :], logits[:, :, :], top_b, ALU.subtract).then_inc(below_done, 1)
            chain(nc.vector.tensor_tensor(is_top[:, :, :], logits[:, :, :], top_b, ALU.is_equal))
            chain(nc.vector.tensor_tensor(rank_of_top[:, :, :], is_top[:, :, :],
                                          const("expert_rank").unsqueeze(1).broadcast_to(te), ALU.mult))
            chain(nc.vector.tensor_reduce(best_rank[:, :], rank_of_top[:, :, :], AX.X, ALU.max))
            nc.vector.tensor_tensor(chosen[:, :, :], rank_of_top[:, :, :],
                                    best_rank[:, :].unsqueeze(2).broadcast_to(te), ALU.is_equal).then_inc(chosen_done, 1)
            dve.wait_ge(powers_done, 1)
            chain(nc.vector.tensor_reduce(power_sum[:, :], powers[:, :, :], AX.X, ALU.add))
            nc.vector.reciprocal(top_weight[:, :], power_sum[:, :]).then_inc(weight_done, 1)

            dve.wait_ge(chosen_done, 1)
            dve.wait_ge(ranks_done, 1)
            et = [P, EXPERTS, TILES]
            chain(nc.vector.tensor_copy(counts[:, :, :], bank_k[:, 0:P].rearrange("p (t e) -> p e t", e=EXPERTS)))
            chain(nc.vector.tensor_tensor_scan(
                counts_to[:, :, :].rearrange("p e t -> p (e t)"), const("not_first_tile"),
                counts[:, :, :].rearrange("p e t -> p (e t)"), 0.0, ALU.mult, ALU.add))
            chain(nc.vector.tensor_tensor(tiles_used[:, :, :], counts_to[:, :, TILES - 1:TILES].broadcast_to(et),
                                          const("tile_edge").unsqueeze(1).broadcast_to(et), ALU.is_gt))
            chain(nc.vector.tensor_reduce(n_tiles[:, :], tiles_used[:, :, :], AX.X, ALU.add))
            chain(nc.vector.tensor_tensor_scan(end_tile[:, :], const("ones")[:, 0:EXPERTS], n_tiles[:, :],
                                               0.0, ALU.mult, ALU.add))
            se = [P, SLOT_TILES, EXPERTS]
            chain(nc.vector.tensor_tensor(past_end[:, :, :],
                                          const("iota")[:, 0:SLOT_TILES].unsqueeze(2).broadcast_to(se),
                                          end_tile[:, :].unsqueeze(1).broadcast_to(se), ALU.is_ge))
            chain(nc.vector.tensor_reduce(tile_expert_f[:, :], past_end[:, :, :], AX.X, ALU.add))
            chain(nc.vector.tensor_scalar(tile_expert[:, :], tile_expert_f[:, :], float(EXPERTS - 1), None, ALU.min))
            chain(nc.vector.tensor_tensor(base[:, :], end_tile[:, :], n_tiles[:, :], ALU.subtract))
            chain(nc.vector.tensor_tensor(counts_before[:, :, :], counts_to[:, :, :], counts[:, :, :], ALU.subtract))
            chain(nc.vector.scalar_tensor_tensor(out=counts_to[:, :, :], in0=base[:, :].unsqueeze(2).broadcast_to(et),
                                                 scalar=float(P), in1=counts_before[:, :, :],
                                                 op0=ALU.mult, op1=ALU.add))
            chain(nc.vector.tensor_tensor(place[:, :, :], bank_q[:, 0:P].rearrange("p (t e) -> p t e", e=EXPERTS),
                                          counts_to[:, :, :].rearrange("p e t -> p t e"), ALU.add))
            chain(nc.vector.tensor_tensor(place_chosen[:, :, :], place[:, :, :], chosen[:, :, :], ALU.mult))
            chain(nc.vector.tensor_reduce(slot[:, :], place_chosen[:, :, :], AX.X, ALU.add))
            chain(nc.vector.tensor_copy(slot_i[:, :], slot[:, :]))
            nc.vector.tensor_scalar(slot_parts_i[:, 0, :], slot_i[:, :], 7, None, ALU.logical_shift_right)
            chain(nc.vector.tensor_scalar(slot_parts_i[:, 1, :], slot_i[:, :], P - 1, None, ALU.bitwise_and))
            chain(nc.vector.tensor_copy(slot_parts[:, :, :], slot_parts_i[:, :, :]))
            ts = [P, TILES, SLOT_TILES]
            for t in range(TILES):
                nc.vector.tensor_scalar(in_lane[:, t, :], iota_b[:, :], slot_parts[:, 1, t:t + 1], None, ALU.is_equal)
            chain(nc.vector.tensor_tensor(in_tile[:, :, 2, :], slot_parts[:, 0, :].unsqueeze(2).broadcast_to(ts),
                                          const("iota")[:, 0:SLOT_TILES].unsqueeze(1).broadcast_to(ts), ALU.is_equal))
            nc.vector.tensor_tensor(in_tile[:, :, 0, :], in_tile[:, :, 2, :],
                                    const("tile_no").unsqueeze(2).broadcast_to(ts), ALU.mult)
            nc.vector.tensor_scalar(in_tile[:, :, 1, :], in_tile[:, :, 2, :], const("partition"), None, ALU.mult
                                    ).then_inc(lanes_done, 1)
            dve.wait_ge(inverse_done, 1)
            chain(nc.vector.tensor_copy(inverse[:, :, :], bank_gv[:, 0:3 * SLOT_TILES].rearrange("p (a s) -> p a s", a=3)))
            chain(nc.vector.scalar_tensor_tensor(out=source[:, :], in0=inverse[:, 0, :], scalar=float(P),
                                                 in1=inverse[:, 1, :], op0=ALU.mult, op1=ALU.add))
            chain(nc.vector.scalar_tensor_tensor(out=target[:, :], in0=inverse[:, 2, :], scalar=-float(NO_TOKEN),
                                                 in1=source[:, :], op0=ALU.mult, op1=ALU.add))
            nc.vector.tensor_scalar(indices[:, 1, :], target[:, :], float(NO_TOKEN), None, ALU.add)
            nc.vector.tensor_copy(indices[:, 0, :], source[:, :]).then_inc(indices_done, 1)

            dve.wait_ge(expert_w_in, 64)
            dve.wait_ge(indices_done, 1)

            def fetch_w1(i, r):
                e = dve.value_load(tile_expert[0:1, bass.ds(i, 1)], min_val=0, max_val=EXPERTS - 1)
                dve.wait_ge(hidden_done, START + i - 1)
                nc.vector.tensor_copy(w1_now[r][:, :], w1_all[:, bass.ds(e * HIDDEN, HIDDEN)]).then_inc(w1_copied, 1)

            def copy_slotT(i, r):
                dve.wait_ge(slotT_done, i + 1)
                dve.wait_ge(hidden_done, START + i - 1)
                nc.vector.tensor_copy(slotT[r][:, :], bank_s[r][:, 0:P]).then_inc(slotT_copied, 1)

            def finish(i, r, u):
                e = dve.value_load(tile_expert[0:1, bass.ds(i, 1)], min_val=0, max_val=EXPERTS - 1)
                dve.wait_ge(y_done, START + i + 1)
                nc.vector.tensor_tensor(y_bias[r][:, :], bank_o[r][:, 0:D], b2_all[:, bass.ds(e * D, D)], ALU.add
                                        ).then_inc(y_biased, 1)
                dve.wait_ge(y_biased, START + i + 1)
                nc.vector.scalar_tensor_tensor(out=got_rows[u][:, 0:D], in0=y_bias[r][:, :],
                                               scalar=got_rows[u][:, 2 * D:ROW], in1=got_rows[u][:, D:2 * D],
                                               op0=ALU.mult, op1=ALU.add).then_inc(out_done, 1)

            for i in range(2):
                fetch_w1(i, i)
                copy_slotT(i, i)
            for i in range(SLOT_TILES):
                if i + 2 < SLOT_TILES:
                    fetch_w1(i + 2, i % 2)
                    copy_slotT(i + 2, i % 2)
                finish(i, i % 2, i % RING)

        @block.tensor
        def _(pe):
            mm = nc.tensor.matmul
            ident = const("ident")

            def keep_warm(n):
                for _ in range(n):
                    mm(bank_s[0][:, :], warm[:, 0:P], warm[:, :], start=True, stop=True)

            pe.wait_ge(warm_zeroed, 1)
            keep_warm(11)
            pe.wait_ge(consts_in, 16)
            pe.wait_ge(attn_w_in, 16)
            mm(bank_gv[:, 0:P], wat[:, 4, :], const("centre"), start=True, stop=True).then_inc(wv_done, 1)

            def turn(m, r, round_):
                pe.wait_ge(xn_done, m + 1)
                pe.wait_ge(ctx_ld[r], 16 * (round_ + 1))
                pe.wait_ge(xcT_done, m)
                for s, src in enumerate((xn[r], ctx_in[r])):
                    for j in range(2):
                        at = s * UNIT + j * P
                        last = nc.tensor.transpose(bank_t[:, at:at + P], src[:, j, :], ident)
                last.then_inc(xT_done, 1)

            def project_qk(m, r):
                pe.wait_ge(xcT_done, m + 1)
                for bank, w, src, free, done in ((bank_q, 0, 0, q_rotated, q_done), (bank_k, 2, UNIT, k_rotated, k_done)):
                    pe.wait_ge(free, m)
                    for s in range(2):
                        last = mm(bank[:, s * UNIT:s * UNIT + UNIT], wat[:, w + s, :], xcT[r][:, src:src + UNIT],
                                  start=True, stop=True)
                    last.then_inc(done, 1)

            def project_gv(m, r):
                pe.wait_ge(gv_copied, m)
                mm(bank_gv[:, 0:UNIT], wat[:, 5, :], xcT[r][:, 0:UNIT], start=True, stop=True)
                for j in range(2):
                    last = mm(bank_gv[:, UNIT + P * j:UNIT + P * j + P],
                              xcT[r][:, UNIT + P * j:UNIT + P * j + P], w_v[:, :], start=True, stop=True)
                last.then_inc(gv_done, 1)

            def scores(m, r, j):
                if j == 0:
                    pe.wait_ge(qh_done, START + m + 1)
                    pe.wait_ge(kg_done, START + m + 1)
                for gp in range(2):
                    pe.wait_ge(sim_done, START + 4 * m + 2 * j + gp - 1)
                    for b in range(2):
                        for gi in range(2):
                            at = j * P + b * SEQ
                            last = mm(bank_s[gp][SEQ * b:SEQ * b + SEQ, 256 * gi:256 * gi + 256],
                                      k_groups[r][:, 2 * gp + gi, at:at + SEQ],
                                      q_heads[r][:, 2 * j + b, :, :].rearrange("p h i -> p (h i)"),
                                      start=True, stop=True)
                    last.then_inc(scores_done, 1)

            def products(m, r, j):
                tile = 2 * m + j
                if j == 0:
                    pe.wait_ge(gv_copied, m + 1)
                pe.wait_ge(sim_done, START + 4 * m + 2 * j + 2)
                pe.wait_ge(ret_done, START + tile)
                for b in range(2):
                    for g in range(GROUPS):
                        last = mm(bank_o[j][Q * g:Q * g + Q, 256 * b:256 * b + 256],
                                  v_batches[r][:, j, b, Q * g:Q * g + Q],
                                  sim[j][:, g // 2, 256 * (g % 2):256 * (g % 2) + 256], start=True, stop=True)
                last.then_inc(av_done, 1)

            def unit(m, r, next_round, more=True):
                if more:
                    turn(m + 1, 1 - r, next_round)
                scores(m, r, 0)
                if more:
                    project_qk(m + 1, 1 - r)
                products(m, r, 0)
                scores(m, r, 1)
                if more:
                    project_gv(m + 1, 1 - r)
                products(m, r, 1)

            keep_warm(2)
            turn(0, 0, 0)
            project_qk(0, 0)
            pe.wait_ge(wv_copied, 1)
            project_gv(0, 0)
            with pe.Fori(0, (UNITS - 2) // 2) as n:
                unit(2 * n, 0, n)
                unit(2 * n + 1, 1, n + 1)
            unit(UNITS - 2, 0, UNITS // 2 - 1)
            unit(UNITS - 1, 1, 0, more=False)

            pe.wait_ge(late_consts_in, 16)
            pe.wait_ge(xcT_done, UNITS)
            for c in range(4):
                pe.wait_ge(squared, c + 1)
                last = mm(bank_t[Q * c:Q * c + Q, :], const("head_mean"), squares[:, QUARTER * c:QUARTER * c + QUARTER],
                          start=True, stop=True)
            last.then_inc(hvar_done, 1)

            def spread(c):
                if c >= 2:
                    pe.wait_ge(attn_done, c - 1)
                mm((bank_q, bank_k)[c % 2][:, :], const("spread", 4)[:, c, :], head_rstd[:, :],
                   start=True, stop=True).then_inc(spread_done, 1)

            def project_out(c):
                pe.wait_ge(attn_done, c + 1)
                if c >= 2:
                    pe.wait_ge(x1_done, c - 1)
                for t in range(QT):
                    last = mm(bank_o[c % 2][:, P * t:P * t + P], attn[c % 2][:, P * t:P * t + P], wat[:, 6, :],
                              start=True, stop=True)
                last.then_inc(proj_done, 1)

            def turn_xn2(c):
                pe.wait_ge(xn2_done, c + 1)
                if c >= 2:
                    pe.wait_ge(xn2T_copied, c - 1)
                for t in range(QT):
                    last = nc.tensor.transpose(bank_s[c % 2][:, P * t:P * t + P], rows[:, QT * c + t, 0:D], ident)
                last.then_inc(xn2T_done, 1)

            def route(c):
                pe.wait_ge(xn2T_copied, c + 1)
                return mm(bank_gv[Q * c:Q * c + Q, :], router_w[:, :], xn2T[:, QUARTER * c:QUARTER * c + QUARTER],
                          start=True, stop=True)

            pe.wait_ge(bias_in, 64)
            pe.wait_ge(hrstd_done, 1)
            spread(0)
            spread(1)
            for c in range(4):
                project_out(c)
                if c + 2 < 4:
                    spread(c + 2)
                if c >= 2:
                    turn_xn2(c - 2)
                if c >= 3:
                    route(c - 3)
            turn_xn2(2)
            route(1)
            turn_xn2(3)
            route(2)
            route(3).then_inc(logitsT_done, 1)
            pe.wait_ge(logitsT_copied, 1)
            for k in range(QT):
                last = nc.tensor.transpose(bank_t[:, P * k:P * k + P], logitsT[:, P * k:P * k + P], ident)
            last.then_inc(logits_turned, 1)
            pe.wait_ge(chosen_done, 1)
            chosen_cols = chosen[:, :, :].rearrange("p t e -> p (t e)")
            mm(bank_q[:, 0:P], const("before"), chosen_cols, start=True, stop=True)
            mm(bank_k[:, 0:P], const("ones"), chosen_cols, start=True, stop=True).then_inc(ranks_done, 1)
            pe.wait_ge(lanes_done, 1)
            for t in range(TILES):
                last = mm(bank_gv[:, 0:3 * SLOT_TILES], in_lane[:, t, :],
                          in_tile[:, t, :, :].rearrange("p a s -> p (a s)"), start=(t == 0), stop=(t == TILES - 1))
            last.then_inc(inverse_done, 1)

            pe.wait_ge(expert_w_in, 64)
            pe.wait_ge(indices_done, 1)

            def turn_rows(i, r, u, round_):
                pe.wait_ge(got[u], 16 * (round_ + 1))
                pe.wait_ge(slotT_copied, START + i - 1)
                nc.tensor.transpose(bank_s[r][:, 0:P], got_rows[u][:, 0:D], ident).then_inc(slotT_done, 1)

            def first_layer(i, r):
                pe.wait_ge(slotT_copied, START + i + 1)
                pe.wait_ge(w1_copied, i + 1)
                pe.wait_ge(silu_done, START + i - 1)
                for c in range(HC):
                    last = mm((bank_q, bank_k)[r][:, P * c:P * c + P], w1_now[r][:, P * c:P * c + P], slotT[r][:, :],
                              start=True, stop=True)
                last.then_inc(hidden_done, 1)

            def second_layer(i, r):
                e = pe.value_load(tile_expert[0:1, bass.ds(i, 1)], min_val=0, max_val=EXPERTS - 1)
                pe.wait_ge(silu_done, START + i + 1)
                pe.wait_ge(y_biased, START + i - 1)
                for c in range(HC):
                    last = mm(bank_o[r][:, 0:D], hiddenT[r][:, c, :], w2_all[:, bass.ds((e * HC + c) * D, D)],
                              start=(c == 0), stop=(c == HC - 1))
                last.then_inc(y_done, 1)

            turn_rows(0, 0, 0, 0)
            turn_rows(1, 1, 1, 0)
            first_layer(0, 0)
            for i in range(SLOT_TILES):
                if i + 2 < SLOT_TILES:
                    turn_rows(i + 2, i % 2, (i + 2) % RING, (i + 2) // RING)
                if i + 1 < SLOT_TILES:
                    first_layer(i + 1, 1 - i % 2)
                second_layer(i, i % 2)


def constants():
    f = np.float32
    p = np.arange(P)
    head, dim = p // HD, p % HD
    pos = np.arange(SEQ)
    even = np.arange(0, HD, 2, dtype=f)
    length_base = ((even + f(0.4 * HD)) / f(1.4 * HD)).astype(f)
    power = (np.arange(-(SEQ // 2), SEQ - SEQ // 2, dtype=f) / f(512.0))[:, None]
    scale = length_base.astype(np.float64)[None, :] ** power.astype(np.float64)
    half = HD // 2
    inv_freq = (1.0 / 10000.0 ** (np.arange(half, dtype=np.float64) / half)).astype(f)
    angle = (pos.astype(f)[:, None] * inv_freq[None, :]).astype(np.float64)
    sin, cos = np.sin(angle), np.cos(angle)
    gamma = 1.0 - np.exp(np.linspace(np.log(1.0 / 32.0), np.log(1.0 / 512.0), HEADS)).astype(f)
    gamma = gamma.astype(f).astype(np.float64)[head][:, None]
    sign = np.where(dim % 2 == 0, -1.0, 1.0)[:, None]
    pair = dim // 2
    up, down = gamma ** pos[None, :], gamma ** -pos[None, :].astype(np.float64)
    tables = [(cos * scale).T[pair] * up, (sin * scale).T[pair] * up * sign,
              (cos / scale).T[pair] * down, (sin / scale).T[pair] * down * sign]
    quad, lane = p // Q, p % Q
    head_mean = np.where(head[:, None] == (np.arange(Q) % HEADS)[None, :], 1.0 / HD, 0.0)
    spread = np.concatenate([((quad == c) & (lane < HEADS))[:, None] * (lane[:, None] == head[None, :])
                             for c in range(4)], axis=1)
    full = {
        "ident": np.eye(P),
        "rotary": np.concatenate(tables, axis=1),
        "causal": (p % SEQ)[:, None] <= pos[None, :],
        "head_in_group": (head % GH)[:, None] == np.arange(GH)[None, :],
        "centre": np.eye(P) - (head[:, None] == head[None, :]) / HD,
        "head_mean": head_mean,
        "spread": spread,
        "before": p[:, None] < p[None, :],
        "ones": np.ones((P, P)),
        "iota": np.tile(p, (P, 1)),
        "tile_no": np.tile(np.arange(TILES), (P, 1)),
        "expert_rank": np.tile(EXPERTS - np.arange(EXPERTS), (P, 1)),
        "tile_edge": np.tile(P * np.arange(TILES), (P, 1)),
        "not_first_tile": np.tile(np.arange(EXPERTS * TILES) % TILES != 0, (P, 1)),
        "partition": p[:, None],
    }
    out = np.zeros((P, CONST_WIDTH), f)
    for name, _ in CONST_PARTS:
        at, width = CONST_AT[name]
        out[:, at:at + width] = full[name]
    return out


def kernel(x, ctx_1024, L0_xattn_W_Q, L0_xattn_W_K, L0_xattn_W_V, L0_xattn_g_w, L0_xattn_g_b, L0_xattn_out_w,
           L0_xattn_out_b, L0_ffn_Wg, L0_ffn_bg, L0_ffn_W1, L0_ffn_b1, L0_ffn_W2, L0_ffn_b2):
    import concourse.bacc as bacc
    from concourse.bass_utils import run_bass_kernel_spmd

    def per_head(w):
        return np.asarray(w).transpose(1, 0, 2).reshape(D, D)

    swap = np.arange(D) ^ 1
    w_q, w_k, w_v = per_head(L0_xattn_W_Q), per_head(L0_xattn_W_K), per_head(L0_xattn_W_V)
    stacked = [w_q, w_q[:, swap], w_k, w_k[:, swap], w_v.T, np.asarray(L0_xattn_g_w).T, np.asarray(L0_xattn_out_w).T]
    router = np.zeros((D, Q), np.float32)
    router[:, :EXPERTS] = np.asarray(L0_ffn_Wg)
    arrays = {
        "x": np.asarray(x).reshape(TOKENS, D),
        "ctx": np.asarray(ctx_1024).reshape(TOKENS, D),
        "w_attn": np.stack(stacked, axis=1),
        "g_b": np.asarray(L0_xattn_g_b).reshape(D, 1),
        "out_b": np.asarray(L0_xattn_out_b),
        "w_gate": router,
        "b_gate": np.asarray(L0_ffn_bg),
        "w1": np.asarray(L0_ffn_W1).transpose(1, 0, 2).reshape(D, EXPERTS * HIDDEN),
        "b1": np.asarray(L0_ffn_b1).reshape(EXPERTS * HC, P).T,
        "w2": np.asarray(L0_ffn_W2).reshape(EXPERTS, HC, P, D).transpose(2, 0, 1, 3).reshape(P, EXPERTS * HC * D),
        "b2": np.asarray(L0_ffn_b2).reshape(EXPERTS * D),
        "consts": constants(),
    }
    nc = bacc.Bacc("TRN2", target_bir_lowering=False, num_devices=1)
    args, ins = [], {}
    for name, a in arrays.items():
        ins[f"in_{name}"] = np.ascontiguousarray(a)
        args.append(nc.dram_tensor(f"in_{name}", a.shape, mybir.dt.from_np(a.dtype), kind="ExternalInput").ap())
    out = nc.dram_tensor("out", (TOKENS, D), F32, kind="ExternalOutput").ap()
    build(nc, *args, out)
    result = run_bass_kernel_spmd(nc, [ins], core_ids=[0])
    return result.results[0]["out"].reshape(BATCH, SEQ, D)
```

```python
from contextlib import ExitStack

import numpy as np
import concourse.bass as bass
from concourse import mybir

F32 = mybir.dt.float32
BF16 = mybir.dt.bfloat16
F16 = mybir.dt.float16
I32 = mybir.dt.int32
ALU = mybir.AluOpType
ACT = mybir.ActivationFunctionType
AX = mybir.AxisListType

P = 128
BATCH, SEQ, D = 32, 64, 128
HEADS, HD = 16, 8
TOKENS = BATCH * SEQ
TILES = TOKENS // P
UNIT = 2 * P
UNITS = TOKENS // UNIT
UB = UNIT // SEQ
GROUPS = 4
GH = HEADS // GROUPS
Q = 32
QUARTER = TOKENS // 4
QT = TILES // 4
EXPERTS, HIDDEN = 8, 512
HC = HIDDEN // P
SLOT_TILES = TILES + EXPERTS - 1
ROW = 2 * D + 1
EPS = 1e-5
RING = 12
NO_TOKEN = 1 << 16

CONST_PARTS = [("ident", P), ("rotary", 4 * SEQ), ("causal", SEQ), ("head_in_group", GH),
               ("centre", P), ("head_mean", 2 * Q), ("spread", UNITS * P), ("before", P), ("ones", P),
               ("iota", P), ("token_number", TILES), ("expert_rank", EXPERTS),
               ("tile_edge", TILES), ("not_first_tile", EXPERTS * TILES)]
CONST_AT, _at = {}, 0
for _name, _width in CONST_PARTS:
    CONST_AT[_name] = (_at, _width)
    _at += _width
CONST_WIDTH = _at
EARLY_CONSTS = CONST_AT["head_mean"][0]
ATTN_WEIGHTS = ["q", "q_pair_swapped", "k", "k_pair_swapped", "v_transposed", "gate", "out"]


def build(nc, x, ctx, w_attn, g_b, out_b, w_gate, b_gate, w1, b1, w2, b2, consts, out):
    stack = ExitStack()
    with stack:
        def sb(name, shape, dt=F32):
            return stack.enter_context(nc.sbuf_tensor(name, shape, dt))

        def bank(name):
            return stack.enter_context(nc.psum_tensor(name, [P, 512], F32))

        def sem(name):
            return stack.enter_context(nc.semaphore(name))

        token_rows = nc.dram_tensor("token_rows", [TOKENS, ROW], F32, kind="Internal").ap()

        cst = sb("cst", [P, CONST_WIDTH])
        wat = sb("wat", [P, len(ATTN_WEIGHTS), P])
        w_v = sb("w_v", [P, P])
        warm = sb("warm", [P, 512], BF16)
        unused = sb("unused", [P, 4])
        gate_bias = sb("gate_bias", [P, 1])
        out_bias = sb("out_bias", [P, D])
        router_bias = sb("router_bias", [P, 1])
        router_w = sb("router_w", [P, Q])
        w1_all = sb("w1_all", [P, EXPERTS * HIDDEN])
        w2_all = sb("w2_all", [P, EXPERTS * HC * D])
        b1_all = sb("b1_all", [P, EXPERTS * HC])
        b2_all = sb("b2_all", [P, EXPERTS * D])
        x_all = sb("x_all", [P, TILES, D])
        x_plus_b = sb("x_plus_b", [P, TILES, D])
        stats = sb("stats", [P, TILES, 6])
        mean_var = sb("mean_var", [P, TILES, 2])
        std = sb("std", [P, TILES])
        rstd = sb("rstd", [P, TILES])
        xn = [sb(f"xn{r}", [P, 2, D]) for r in range(2)]
        ctx_in = [sb(f"ctx_in{r}", [P, 2, D]) for r in range(2)]
        xcT = [sb(f"xcT{r}", [P, 2 * UNIT]) for r in range(2)]
        q_parts = sb("q_parts", [P, 2, UNIT])
        k_parts = sb("k_parts", [P, 2, UNIT])
        q_sum = [sb(f"q_sum{r}", [P, UNIT]) for r in range(2)]
        k_sum = [sb(f"k_sum{r}", [P, UNIT]) for r in range(2)]
        q_heads = [sb(f"q_heads{r}", [P, UB, GH, SEQ]) for r in range(2)]
        k_groups = [sb(f"k_groups{r}", [P, GROUPS, UNIT]) for r in range(2)]
        v_batches = [sb(f"v_batches{r}", [P, 2, 2, P]) for r in range(2)]
        sim = [sb(f"sim{j}", [P, 2, 512]) for j in range(2)]
        ret_sum = [sb(f"ret_sum{j}", [P, GH - 1, P]) for j in range(2)]
        retT = sb("retT", [P, TOKENS])
        gateT = sb("gateT", [P, TOKENS])
        ret_gate = sb("ret_gate", [P, TOKENS])
        squares = x_all[:, :, :].rearrange("p t d -> p (t d)")
        head_var = sb("head_var", [P, UNIT])
        head_std = sb("head_std", [P, UNIT])
        head_rstd = sb("head_rstd", [P, UNIT])
        attn = [sb(f"attn{r}", [P, QUARTER]) for r in range(2)]
        rows = sb("rows", [P, TILES, 2 * D])
        stats2 = sb("stats2", [P, TILES, 6])
        mean_var2 = sb("mean_var2", [P, TILES, 2])
        var_eps2 = sb("var_eps2", [P, TILES])
        std2 = sb("std2", [P, TILES])
        rstd2 = sb("rstd2", [P, TILES])
        shift2 = sb("shift2", [P, TILES])
        xn2T = retT
        logitsT = sb("logitsT", [P, 512])
        te = [P, TILES, EXPERTS]
        top = sb("top", [P, TILES])
        below_top = sb("below_top", te)
        powers = sb("powers", te)
        power_sum = sb("power_sum", [P, TILES])
        top_weight = sb("top_weight", [P, TILES])
        rank_of_top = sb("rank_of_top", te)
        best_rank = sb("best_rank", [P, TILES])
        chosen = sb("chosen", te, BF16)
        counts_to = sb("counts_to", [P, EXPERTS, TILES])
        tiles_used = sb("tiles_used", [P, EXPERTS, TILES])
        n_tiles = sb("n_tiles", [P, EXPERTS])
        end_tile = sb("end_tile", [P, EXPERTS])
        base = sb("base", [P, EXPERTS])
        counts_before = sb("counts_before", [P, EXPERTS, TILES])
        place = sb("place", te)
        place_b = sb("place_b", te)
        place_chosen = sb("place_chosen", te)
        slot = sb("slot", [P, TILES])
        slot_i = sb("slot_i", [P, TILES], I32)
        slot_parts_i = sb("slot_parts_i", [P, 2, TILES], I32)
        slot_parts = sb("slot_parts", [P, 2, TILES])
        past_end = sb("past_end", [P, SLOT_TILES, EXPERTS])
        tile_expert_f = sb("tile_expert_f", [P, SLOT_TILES])
        tile_expert = sb("tile_expert", [P, SLOT_TILES], I32)
        is_tile = sb("is_tile", [P, TILES, SLOT_TILES], F16)
        in_tile = sb("in_tile", [P, TILES, SLOT_TILES], F16)
        in_lane = sb("in_lane", [P, TILES, P], F16)
        iota_h = sb("iota_h", [P, P], F16)
        before_ones = sb("before_ones", [P, 2, P], BF16)
        no_token = sb("no_token", [P, SLOT_TILES])
        indices = sb("indices", [P, 2, SLOT_TILES], I32)
        got_rows = [sb(f"got_rows{u}", [P, ROW]) for u in range(RING)]
        slotT = [sb(f"slotT{r}", [P, P]) for r in range(2)]
        w1_now = [sb(f"w1_now{r}", [P, HIDDEN]) for r in range(2)]
        hiddenT = [sb(f"hiddenT{r}", [P, HC, P]) for r in range(2)]
        y_bias = [sb(f"y_bias{r}", [P, D]) for r in range(2)]

        bank_t, bank_q, bank_k, bank_gv = (bank(f"bank_{n}") for n in ("t", "q", "k", "gv"))
        bank_s = [bank(f"bank_s{i}") for i in range(2)]
        bank_o = [bank(f"bank_o{i}") for i in range(2)]

        def const(name, *dims):
            at, width = CONST_AT[name]
            part = cst[:, at:at + width]
            if dims:
                part = part.rearrange("p (a b) -> p a b", a=dims[0])
            return part

        consts_in, late_consts_in, attn_w_in, bias_in, expert_w_in = map(
            sem, ("consts_in", "late_consts_in", "attn_w_in", "bias_in", "expert_w_in"))
        x_in = [sem(f"x_in{c}") for c in range(4)]
        ctx_ld = [sem(f"ctx_ld{r}") for r in range(2)]
        zeroed, warm_zeroed = map(sem, ("zeroed", "warm_zeroed"))
        xb_done = sem("xb_done")
        dve_step = sem("dve_step")
        var_done, std_done, rstd_done = map(sem, ("var_done", "std_done", "rstd_done"))
        wv_done, wv_copied = map(sem, ("wv_done", "wv_copied"))
        xn_done, xT_done, xcT_done = map(sem, ("xn_done", "xT_done", "xcT_done"))
        q_done, k_done, gv_done = map(sem, ("q_done", "k_done", "gv_done"))
        q_rotated, k_rotated, q_summed, k_summed = map(sem, ("q_rotated", "k_rotated", "q_summed", "k_summed"))
        qh_done, kg_done, gv_copied = map(sem, ("qh_done", "kg_done", "gv_copied"))
        scores_done, sim_done, av_done = map(sem, ("scores_done", "sim_done", "av_done"))
        head0_done, head_added, ret_done = map(sem, ("head0_done", "head_added", "ret_done"))
        squared, ret_gated, hvar_done, hvar_eps, hstd_done, hrstd_done = map(
            sem, ("squared", "ret_gated", "hvar_done", "hvar_eps", "hstd_done", "hrstd_done"))
        spread_done, attn_done, proj_done, x1_done = map(sem, ("spread_done", "attn_done", "proj_done", "x1_done"))
        var2_done, std2_done, rstd2_done, xn2_done, xn2T_done, xn2T_copied = map(
            sem, ("var2_done", "std2_done", "rstd2_done", "xn2_done", "xn2T_done", "xn2T_copied"))
        logitsT_done, logitsT_copied, logits_turned = map(sem, ("logitsT_done", "logitsT_copied", "logits_turned"))
        below_done, powers_done, weight_done = map(sem, ("below_done", "powers_done", "weight_done"))
        converted, chosen_done, ranks_done, slots_done, lanes_done = map(
            sem, ("converted", "chosen_done", "ranks_done", "slots_done", "lanes_done"))
        is_tile_done, in_tile_done, inverse_done, indices_done, targets_done = map(
            sem, ("is_tile_done", "in_tile_done", "inverse_done", "indices_done", "targets_done"))
        rows_out, weights_out = map(sem, ("rows_out", "weights_out"))
        got = [sem(f"got{u}") for u in range(RING)]
        scattered = [sem(f"scattered{u}") for u in range(RING)]
        slotT_done, slotT_copied, w1_copied = map(sem, ("slotT_done", "slotT_copied", "w1_copied"))
        hidden_done, silu_done, y_done, y_biased, out_done = map(
            sem, ("hidden_done", "silu_done", "y_done", "y_biased", "out_done"))

        START = 4 + 1
        ring_counts = [xT_done, gv_done, scores_done, av_done, ret_done, sim_done, kg_done, qh_done,
                       slotT_copied, hidden_done, silu_done, y_done, y_biased]

        block = stack.enter_context(nc.Block())

        @block.sync
        def _(sp):
            x_tiles = x.rearrange("(t p) d -> p t d", p=P)
            ctx_units = ctx.rearrange("(m j p) d -> m p j d", p=P, j=2)

            def load_ctx(m, r):
                sp.wait_ge(xT_done, START + m - 1)
                sp.dma_start(ctx_in[r][:, :, :],
                             ctx_units[m] if isinstance(m, int)
                             else ctx_units[bass.ds(m, 1)].rearrange("m p j d -> (m p) j d")
                             ).then_inc(ctx_ld[r], 16)

            for c in range(4):
                sp.dma_start(x_all[:, QT * c:QT * c + QT, :], x_tiles[:, QT * c:QT * c + QT, :]).then_inc(x_in[c], 16)
                if c == 0:
                    load_ctx(0, 0)
                    sp.dma_start(wat[:, :, :], w_attn).then_inc(attn_w_in, 16)
            load_ctx(1, 1)
            sp.dma_start(out_bias[:, :], out_b.partition_broadcast(P)).then_inc(bias_in, 16)
            sp.dma_start(router_bias[:, :], b_gate).then_inc(bias_in, 16)
            sp.dma_start(router_w[:, :], w_gate).then_inc(bias_in, 16)
            sp.dma_start(cst[:, EARLY_CONSTS:CONST_WIDTH], consts[:, EARLY_CONSTS:CONST_WIDTH]).then_inc(late_consts_in, 16)
            for m in range(2, UNITS):
                load_ctx(m, m % 2)
            sp.dma_start(w1_all[:, :], w1).then_inc(expert_w_in, 16)
            sp.dma_start(w2_all[:, :], w2).then_inc(expert_w_in, 16)
            sp.dma_start(b1_all[:, :], b1).then_inc(expert_w_in, 16)
            sp.dma_start(b2_all[:, :], b2.partition_broadcast(P)).then_inc(expert_w_in, 16)
            row_tiles = token_rows.rearrange("(t p) r -> p t r", p=P)
            for c in range(4):
                sp.wait_ge(xn2_done, c + 1)
                sp.dma_start(row_tiles[:, QT * c:QT * c + QT, 0:2 * D], rows[:, QT * c:QT * c + QT, :]
                             ).then_inc(rows_out, 16)
            sp.wait_ge(weight_done, 1)
            with nc.allow_non_contiguous_dma(reason="one weight per token"):
                sp.dma_start(row_tiles[:, :, 2 * D:ROW], top_weight[:, :].unsqueeze(2)).then_inc(weights_out, 16)

        @block.gpsimd
        def _(pool):
            for count in ring_counts:
                pool.sem_inc(count, START)
            for r in range(2):
                pool.memset(k_groups[r][:, :, :], 0.0).then_inc(zeroed, 1)
                pool.memset(v_batches[r][:, :, :, :], 0.0).then_inc(zeroed, 1)

            def add_k(m, r):
                pool.wait_ge(k_rotated, m + 1)
                pool.wait_ge(kg_done, START + m - 1)
                pool.tensor_tensor(k_sum[r][:, :], k_parts[:, 0, :], k_parts[:, 1, :], ALU.add).then_inc(k_summed, 1)

            add_k(0, 0)
            pool.wait_ge(bias_in, 64)
            for c in range(4):
                pool.wait_ge(x_in[c], 16)
                tiles = slice(QT * c, QT * c + QT)
                pool.tensor_tensor(x_plus_b[:, tiles, :], x_all[:, tiles, :],
                                   out_bias[:, :].unsqueeze(1).broadcast_to([P, QT, D]), ALU.add).then_inc(xb_done, 1)
                if c == 0:
                    add_k(1, 1)
            with pool.Fori(0, (UNITS - 2) // 2) as n:
                for r in range(2):
                    add_k(2 * n + 2 + r, r)
            for c in range(4):
                cols = slice(QUARTER * c, QUARTER * c + QUARTER)
                pool.wait_ge(ret_done, START + QT * (c + 1))
                pool.wait_ge(gv_copied, 2 * (c + 1))
                pool.tensor_tensor(ret_gate[:, cols], retT[:, cols], gateT[:, cols], ALU.mult).then_inc(ret_gated, 1)

            ts = [P, TILES, SLOT_TILES]
            pool.wait_ge(late_consts_in, 16)
            pool.wait_ge(is_tile_done, 1)
            pool.tensor_tensor(in_tile[:, :, :], is_tile[:, :, :], const("token_number").unsqueeze(2).broadcast_to(ts),
                               ALU.mult).then_inc(in_tile_done, 1)

            last_row = pool.to_reg(TOKENS - 1)
            pool.wait_ge(indices_done, 1)
            pool.wait_ge(rows_out, 64)
            pool.wait_ge(weights_out, 16)


            def gather(i):
                u = i % RING
                if i >= RING:
                    pool.wait_ge(scattered[u], 16 * (i // RING))
                pool.indirect_dma_start(out=got_rows[u][:, :], out_offset=None, in_=token_rows[:, :],
                                        in_offset=bass.IndirectOffsetOnAxis(ap=indices[:, 0, i:i + 1], axis=0),
                                        bounds_check=last_row, oob_is_err=False).then_inc(got[u], 16)

            def scatter(i):
                pool.wait_ge(out_done, i + 1)
                if i == 0:
                    pool.wait_ge(targets_done, 1)
                pool.indirect_dma_start(out=out[:, :],
                                        out_offset=bass.IndirectOffsetOnAxis(ap=indices[:, 1, i:i + 1], axis=0),
                                        in_=got_rows[i % RING][:, 0:D], in_offset=None,
                                        bounds_check=last_row, oob_is_err=False).then_inc(scattered[i % RING], 16)

            AHEAD = RING - 2
            for i in range(AHEAD):
                gather(i)
            for i in range(SLOT_TILES):
                if i + AHEAD < SLOT_TILES:
                    gather(i + AHEAD)
                scatter(i)
            for u in range(RING):
                pool.wait_ge(scattered[u], 16 * len(range(u, SLOT_TILES, RING)))

        @block.scalar
        def _(act):
            act.dma_start(cst[:, 0:EARLY_CONSTS], consts[:, 0:EARLY_CONSTS]).then_inc(consts_in, 16)
            act.wait_ge(warm_zeroed, 1)
            nc.scalar.activation(unused[:, 0:1], warm[:, 0:1], ACT.Sqrt)
            act.dma_start(gate_bias[:, :], g_b).then_inc(bias_in, 16)
            def roots(tiles, step):
                act.wait_ge(var_done, step)
                nc.scalar.activation(std[:, tiles], rstd[:, tiles], ACT.Sqrt).then_inc(std_done, 1)

            roots(slice(0, QT), 1)
            act.wait_ge(wv_done, 1)
            nc.scalar.activation(w_v[:, :], bank_gv[:, 0:P], ACT.Copy).then_inc(wv_copied, 1)
            head_mask = const("head_in_group")

            def copy_transposed(m, r):
                act.wait_ge(xT_done, START + m + 1)
                act.wait_ge(gv_done, START + m - 1)
                nc.scalar.activation(xcT[r][:, :], bank_t[:, :], ACT.Copy).then_inc(xcT_done, 1)

            def split_q(m, r):
                act.wait_ge(q_summed, m + 1)
                act.wait_ge(scores_done, START + 4 * (m - 1))
                for h in range(GH):
                    last = nc.scalar.activation(q_heads[r][:, :, h, :], q_sum[r][:, :].rearrange("p (b i) -> p b i", b=UB),
                                                ACT.Copy, scale=head_mask[:, h:h + 1])
                last.then_inc(qh_done, 1)

            def split_k(m, r):
                act.wait_ge(k_summed, m + 1)
                act.wait_ge(scores_done, START + 4 * (m - 1))
                for g in range(GROUPS):
                    last = nc.scalar.activation(k_groups[r][Q * g:Q * g + Q, g, :], k_sum[r][Q * g:Q * g + Q, :], ACT.Copy)
                last.then_inc(kg_done, 1)

            def gate_and_values(m, r):
                act.wait_ge(gv_done, START + m + 1)
                act.wait_ge(av_done, START + 2 * (m - 1))
                nc.scalar.activation(gateT[:, bass.ds(m * UNIT, UNIT)], bank_gv[:, 0:UNIT], ACT.Silu,
                                     bias=gate_bias[:, 0:1])
                values = bank_gv[:, UNIT:2 * UNIT].rearrange("p (j f) -> p j f", j=2)
                nc.scalar.activation(v_batches[r][0:64, :, 0, :], values[0:64], ACT.Copy)
                nc.scalar.activation(v_batches[r][64:128, :, 1, :], values[64:128], ACT.Copy).then_inc(gv_copied, 1)

            def first_head(m, j):
                tile = 2 * m + j
                act.wait_ge(av_done, START + tile + 1)
                act.wait_ge(ret_done, START + tile)
                nc.scalar.activation(ret_sum[j][:, 0, :].rearrange("p (b i) -> p b i", b=2),
                                     bank_o[j][:, :].rearrange("p (b h i) -> p b h i", b=2, h=GH)[:, :, 0, :],
                                     ACT.Copy, scale=head_mask[:, 0:1]).then_inc(head0_done, 1)

            def unit(m, r, more=True):
                if more:
                    copy_transposed(m + 1, 1 - r)
                first_head(m, 0)
                if more:
                    split_q(m + 1, 1 - r)
                    split_k(m + 1, 1 - r)
                    gate_and_values(m + 1, 1 - r)
                first_head(m, 1)

            copy_transposed(0, 0)
            act.wait_ge(bias_in, 64)
            act.wait_ge(consts_in, 16)
            act.wait_ge(zeroed, 4)
            roots(slice(QT, TILES), 2)
            nc.scalar.activation(unused[:, 1:2], warm[:, 0:1], ACT.Silu)
            split_q(0, 0)
            gate_and_values(0, 0)
            with act.Fori(0, (UNITS - 2) // 2) as n:
                for r in range(2):
                    unit(2 * n + r, r)
            unit(UNITS - 2, 0)
            unit(UNITS - 1, 1, more=False)

            for c in range(4):
                cols = slice(QUARTER * c, QUARTER * c + QUARTER)
                act.wait_ge(ret_done, START + QT * (c + 1))
                act.wait_ge(xb_done, c + 1)
                nc.scalar.activation(squares[:, cols], retT[:, cols], ACT.Square).then_inc(squared, 1)
            act.wait_ge(hvar_eps, 1)
            nc.scalar.activation(head_std[:, :], head_var[:, :], ACT.Sqrt).then_inc(hstd_done, 1)

            def copy_xn2T(c):
                act.wait_ge(xn2T_done, c + 1)
                nc.scalar.activation(xn2T[:, QUARTER * c:QUARTER * c + QUARTER], bank_s[c % 2][:, :], ACT.Copy
                                     ).then_inc(xn2T_copied, 1)

            act.wait_ge(late_consts_in, 16)
            nc.scalar.activation(before_ones[:, 0, :], const("before"), ACT.Copy).then_inc(converted, 1)
            nc.scalar.activation(before_ones[:, 1, :], const("ones"), ACT.Copy).then_inc(converted, 1)
            nc.scalar.activation(iota_h[:, :], const("iota"), ACT.Copy).then_inc(converted, 1)

            def roots2(c):
                act.wait_ge(var2_done, c + 1)
                nc.scalar.activation(std2[:, QT * c:QT * c + QT], var_eps2[:, QT * c:QT * c + QT], ACT.Sqrt
                                     ).then_inc(std2_done, 1)

            def normalise2(c):
                act.wait_ge(rstd2_done, c + 1)
                for t in range(QT * c, QT * c + QT):
                    last = nc.scalar.activation(rows[:, t, 0:D], rows[:, t, D:2 * D], ACT.Identity,
                                                bias=shift2[:, t:t + 1], scale=rstd2[:, t:t + 1])
                last.then_inc(xn2_done, 1)

            for c in range(4):
                roots2(c)
                normalise2(c)
                if c >= 1:
                    copy_xn2T(c - 1)
            copy_xn2T(3)
            act.wait_ge(logitsT_done, 1)
            nc.scalar.activation(logitsT[:, 0:2 * P], bank_gv[:, 0:2 * P], ACT.Identity, bias=router_bias[:, 0:1]
                                 ).then_inc(logitsT_copied, 1)
            act.wait_ge(below_done, 1)
            nc.scalar.activation(powers[:, :, :], below_top[:, :, :], ACT.Exp).then_inc(powers_done, 1)
            nc.scalar.activation(unused[:, 2:3], warm[:, 0:1], ACT.Silu)

            act.wait_ge(expert_w_in, 64)
            act.wait_ge(indices_done, 1)

            def silu(i, r):
                e = act.value_load(tile_expert[0:1, bass.ds(i, 1)], min_val=0, max_val=EXPERTS - 1)
                act.wait_ge(hidden_done, START + i + 1)
                act.wait_ge(y_done, START + i - 1)
                h_bank = (bank_q, bank_k)[r]
                for c in range(HC):
                    last = nc.scalar.activation(hiddenT[r][:, c, :], h_bank[:, P * c:P * c + P], ACT.Silu,
                                                bias=b1_all[:, bass.ds(e * HC + c, 1)])
                last.then_inc(silu_done, 1)

            for i in range(SLOT_TILES):
                silu(i, i % 2)

        @block.vector
        def _(dve):
            steps = [0]

            def chain(ins):
                steps[0] += 1
                ins.then_inc(dve_step, 1)
                dve.wait_ge(dve_step, steps[0])

            nc.vector.memset(warm[:, :], 0.0).then_inc(warm_zeroed, 1)

            def statistics(first, end):
                for t in range(first, end):
                    if t % QT == 0:
                        dve.wait_ge(x_in[t // QT], 16)
                    last = nc.vector.bn_stats(stats[:, t, :], x_all[:, t, :])
                return last

            def variances(first, end):
                for t in range(first, end):
                    last = nc.vector.bn_aggr(mean_var[:, t, :], stats[:, t, :])
                chain(last)
                nc.vector.tensor_scalar(rstd[:, first:end], mean_var[:, first:end, 1], EPS, None, ALU.add
                                        ).then_inc(var_done, 1)

            def invert_std(first, end, step):
                dve.wait_ge(std_done, step)
                nc.vector.reciprocal(rstd[:, first:end], std[:, first:end]).then_inc(rstd_done, 1)
                dve.wait_ge(rstd_done, step)

            chain(statistics(0, QT))
            variances(0, QT)
            invert_std(0, QT, 1)

            rotary = const("rotary", 4)
            causal = const("causal").unsqueeze(1).broadcast_to([P, 2 * GH, SEQ])
            head_mask = const("head_in_group")

            def normalise(m, r):
                dve.wait_ge(xT_done, START + m - 1)
                for j in range(2):
                    tile = 2 * m + j
                    last = nc.vector.tensor_scalar(
                        xn[r][:, j, :], x_all[:, bass.ds(tile, 1), :].rearrange("p a d -> p (a d)"),
                        mean_var[:, bass.ds(tile, 1), 0:1].rearrange("p a b -> p (a b)"),
                        rstd[:, bass.ds(tile, 1)], ALU.subtract, ALU.mult)
                last.then_inc(xn_done, 1)

            def rotate(parts, bank, table):
                return nc.vector.tensor_tensor(
                    parts[:, :, :].rearrange("p s (b i) -> p s b i", b=UB),
                    bank[:, :].rearrange("p (s b i) -> p s b i", s=2, b=UB),
                    rotary[:, table:table + 2, :].unsqueeze(2).broadcast_to([P, 2, UB, SEQ]), ALU.mult)

            def rotate_qk(m, r):
                dve.wait_ge(q_done, m + 1)
                dve.wait_ge(q_summed, m)
                rotate(q_parts, bank_q, 0).then_inc(q_rotated, 1)
                dve.wait_ge(k_done, m + 1)
                dve.wait_ge(k_summed, m)
                rotate(k_parts, bank_k, 2).then_inc(k_rotated, 1)
                dve.wait_ge(q_rotated, m + 1)
                dve.wait_ge(qh_done, START + m - 1)
                nc.vector.tensor_tensor(q_sum[r][:, :], q_parts[:, 0, :], q_parts[:, 1, :], ALU.add
                                        ).then_inc(q_summed, 1)

            def mask_scores(m, j):
                tile = 2 * m + j
                for gp in range(2):
                    dve.wait_ge(scores_done, START + 4 * m + 2 * j + gp + 1)
                    if gp == 0:
                        dve.wait_ge(av_done, START + tile)
                    nc.vector.tensor_tensor(sim[j][:, gp, :].rearrange("p (h i) -> p h i", i=SEQ),
                                            bank_s[gp][:, :].rearrange("p (h i) -> p h i", i=SEQ),
                                            causal, ALU.mult).then_inc(sim_done, 1)

            def add_heads(m, j):
                tile = 2 * m + j
                products = bank_o[j][:, :].rearrange("p (b h i) -> p b h i", b=2, h=GH)
                dve.wait_ge(head0_done, tile + 1)
                for h in range(1, GH):
                    if h > 1:
                        dve.wait_ge(head_added, 2 * tile + h - 1)
                    before = ret_sum[j][:, h - 1, :].rearrange("p (b i) -> p b i", b=2)
                    after = ret_sum[j][:, h, :] if h < GH - 1 else retT[:, bass.ds(tile * P, P)]
                    ins = nc.vector.scalar_tensor_tensor(
                        out=after.rearrange("p (b i) -> p b i", b=2), in0=products[:, :, h, :],
                        scalar=head_mask[:, h:h + 1], in1=before, op0=ALU.mult, op1=ALU.add)
                    ins.then_inc(head_added if h < GH - 1 else ret_done, 1)

            def unit(m, r, more=1):
                mask_scores(m, 0)
                if more:
                    rotate_qk(m + 1, 1 - r)
                add_heads(m, 0)
                mask_scores(m, 1)
                if more == 2 or more is True:
                    normalise(m + 2, r)
                add_heads(m, 1)

            normalise(0, 0)
            normalise(1, 1)
            chain(statistics(QT, TILES))
            variances(QT, TILES)
            dve.wait_ge(consts_in, 16)
            rotate_qk(0, 0)
            invert_std(QT, TILES, 2)
            dve.wait_ge(k_summed, 1)
            dve.wait_ge(zeroed, 4)
            for g in range(GROUPS):
                last = nc.vector.tensor_copy(k_groups[0][Q * g:Q * g + Q, g, :], k_sum[0][Q * g:Q * g + Q, :])
            last.then_inc(kg_done, 1)
            with dve.Fori(0, (UNITS - 2) // 2) as n:
                for r in range(2):
                    unit(2 * n + r, r, more=2)
            unit(UNITS - 2, 0, more=1)
            unit(UNITS - 1, 1, more=0)

            dve.wait_ge(hvar_done, 1)
            nc.vector.tensor_scalar(head_var[:, :], bank_t[:, 0:UNIT], EPS, None, ALU.add).then_inc(hvar_eps, 1)
            dve.wait_ge(hstd_done, 1)
            nc.vector.reciprocal(head_rstd[:, :], head_std[:, :]).then_inc(hrstd_done, 1)

            def close_attention(c):
                dve.wait_ge(spread_done, c + 1)
                dve.wait_ge(ret_gated, c + 1)
                if c >= 2:
                    dve.wait_ge(proj_done, c - 1)
                nc.vector.tensor_tensor(attn[c % 2][:, :], (bank_q, bank_k)[c % 2][:, :],
                                        ret_gate[:, QUARTER * c:QUARTER * c + QUARTER], ALU.mult
                                        ).then_inc(attn_done, 1)

            def residual(c):
                tiles = slice(QT * c, QT * c + QT)
                dve.wait_ge(proj_done, c + 1)
                dve.wait_ge(xb_done, c + 1)
                nc.vector.tensor_tensor(rows[:, tiles, D:2 * D],
                                        bank_o[c % 2][:, :].rearrange("p (t d) -> p t d", d=D),
                                        x_plus_b[:, tiles, :], ALU.add).then_inc(x1_done, 1)
                dve.wait_ge(x1_done, c + 1)
                for t in range(QT * c, QT * c + QT):
                    last = nc.vector.bn_stats(stats2[:, t, :], rows[:, t, D:2 * D])
                chain(last)
                for t in range(QT * c, QT * c + QT):
                    last = nc.vector.bn_aggr(mean_var2[:, t, :], stats2[:, t, :])
                chain(last)
                nc.vector.tensor_scalar(var_eps2[:, tiles], mean_var2[:, tiles, 1], EPS, None, ALU.add
                                        ).then_inc(var2_done, 1)

            def invert_std2(c):
                tiles = slice(QT * c, QT * c + QT)
                dve.wait_ge(std2_done, c + 1)
                chain(nc.vector.reciprocal(rstd2[:, tiles], std2[:, tiles]))
                nc.vector.scalar_tensor_tensor(out=shift2[:, tiles], in0=mean_var2[:, tiles, 0], scalar=-1.0,
                                               in1=rstd2[:, tiles], op0=ALU.mult, op1=ALU.mult).then_inc(rstd2_done, 1)

            close_attention(0)
            close_attention(1)
            for c in range(4):
                residual(c)
                if c + 2 < 4:
                    close_attention(c + 2)
                invert_std2(c)
            dve.wait_ge(late_consts_in, 16)

            dve.wait_ge(bias_in, 64)
            dve.wait_ge(logitsT_done, 1)
            nc.vector.tensor_scalar(logitsT[:, 2 * P:4 * P], bank_o[0][:, 0:2 * P], router_bias[:, 0:1], None, ALU.add
                                    ).then_inc(logitsT_copied, 1)
            dve.wait_ge(logits_turned, 1)

            def by_quarter(a):
                return a[:, :, :].rearrange("p (c k) e -> p c k e", c=4)

            logits = bank_t[:, :].rearrange("p (k c e) -> p c k e", k=QT, c=4)[:, :, :, 0:EXPERTS]
            chain(nc.vector.tensor_reduce(top[:, :].rearrange("p (c k) -> p c k", c=4), logits, AX.X, ALU.max))
            top_b = top[:, :].rearrange("p (c k) -> p c k", c=4).unsqueeze(3).broadcast_to([P, 4, QT, EXPERTS])
            nc.vector.tensor_tensor(by_quarter(below_top), logits, top_b, ALU.subtract).then_inc(below_done, 1)
            dve.wait_ge(below_done, 1)
            chain(nc.vector.scalar_tensor_tensor(
                out=rank_of_top[:, :, :], in0=below_top[:, :, :], scalar=0.0,
                in1=const("expert_rank").unsqueeze(1).broadcast_to(te), op0=ALU.is_equal, op1=ALU.mult))
            chain(nc.vector.tensor_reduce(best_rank[:, :], rank_of_top[:, :, :], AX.X, ALU.max))
            nc.vector.tensor_tensor(chosen[:, :, :], rank_of_top[:, :, :],
                                    best_rank[:, :].unsqueeze(2).broadcast_to(te), ALU.is_equal).then_inc(chosen_done, 1)
            dve.wait_ge(powers_done, 1)
            chain(nc.vector.tensor_reduce(power_sum[:, :], powers[:, :, :], AX.X, ALU.add))
            nc.vector.reciprocal(top_weight[:, :], power_sum[:, :]).then_inc(weight_done, 1)

            dve.wait_ge(chosen_done, 1)
            dve.wait_ge(ranks_done, 1)
            et = [P, EXPERTS, TILES]
            ranks = bank_q[:, 0:P].rearrange("p (t e) -> p t e", e=EXPERTS)
            counts = bank_k[:, 0:P]
            chain(nc.vector.tensor_tensor_scan(counts_to[:, :, :].rearrange("p e t -> p (e t)"),
                                               const("not_first_tile"), counts, 0.0, ALU.mult, ALU.add))
            chain(nc.vector.tensor_tensor(tiles_used[:, :, :], counts_to[:, :, TILES - 1:TILES].broadcast_to(et),
                                          const("tile_edge").unsqueeze(1).broadcast_to(et), ALU.is_gt))
            nc.vector.tensor_tensor(counts_before[:, :, :], counts_to[:, :, :],
                                    counts.rearrange("p (e t) -> p e t", e=EXPERTS), ALU.subtract)
            chain(nc.vector.tensor_reduce(n_tiles[:, :], tiles_used[:, :, :], AX.X, ALU.add))
            nc.vector.tensor_tensor(place[:, :, :], ranks, counts_before[:, :, :].rearrange("p e t -> p t e"), ALU.add)
            chain(nc.vector.tensor_tensor_scan(end_tile[:, :], const("ones")[:, 0:EXPERTS], n_tiles[:, :],
                                               0.0, ALU.mult, ALU.add))
            chain(nc.vector.tensor_tensor(base[:, :], end_tile[:, :], n_tiles[:, :], ALU.subtract))
            chain(nc.vector.scalar_tensor_tensor(out=place_b[:, :, :], in0=base[:, :].unsqueeze(1).broadcast_to(te),
                                                 scalar=float(P), in1=place[:, :, :], op0=ALU.mult, op1=ALU.add))
            chain(nc.vector.tensor_tensor(place_chosen[:, :, :], place_b[:, :, :], chosen[:, :, :], ALU.mult))
            chain(nc.vector.tensor_reduce(slot[:, :], place_chosen[:, :, :], AX.X, ALU.add))
            chain(nc.vector.tensor_copy(slot_i[:, :], slot[:, :]))
            nc.vector.tensor_scalar(slot_parts_i[:, 0, :], slot_i[:, :], 7, None, ALU.logical_shift_right)
            chain(nc.vector.tensor_scalar(slot_parts_i[:, 1, :], slot_i[:, :], P - 1, None, ALU.bitwise_and))
            nc.vector.tensor_copy(slot_parts[:, :, :], slot_parts_i[:, :, :]).then_inc(slots_done, 1)
            dve.wait_ge(slots_done, 1)
            dve.wait_ge(converted, 3)
            ts = [P, TILES, SLOT_TILES]
            nc.vector.tensor_tensor(is_tile[:, :, :], slot_parts[:, 0, :].unsqueeze(2).broadcast_to(ts),
                                    const("iota")[:, 0:SLOT_TILES].unsqueeze(1).broadcast_to(ts), ALU.is_equal
                                    ).then_inc(is_tile_done, 1)
            for t in range(TILES):
                last = nc.vector.tensor_scalar(in_lane[:, t, :], iota_h[:, :], slot_parts[:, 1, t:t + 1], None,
                                               ALU.is_equal)
            last.then_inc(lanes_done, 1)
            se = [P, SLOT_TILES, EXPERTS]
            chain(nc.vector.tensor_tensor(past_end[:, :, :],
                                          const("iota")[:, 0:SLOT_TILES].unsqueeze(2).broadcast_to(se),
                                          end_tile[:, :].unsqueeze(1).broadcast_to(se), ALU.is_ge))
            chain(nc.vector.tensor_reduce(tile_expert_f[:, :], past_end[:, :, :], AX.X, ALU.add))
            chain(nc.vector.tensor_scalar(tile_expert[:, :], tile_expert_f[:, :], float(EXPERTS - 1), None, ALU.min))
            dve.wait_ge(inverse_done, 1)
            inverse = bank_gv[:, 0:SLOT_TILES]
            nc.vector.tensor_scalar(indices[:, 0, :], inverse, 1.0, 0.0, ALU.subtract, ALU.max).then_inc(indices_done, 1)
            chain(nc.vector.tensor_scalar(no_token[:, :], inverse, 0.0, float(NO_TOKEN), ALU.is_equal, ALU.mult))
            nc.vector.scalar_tensor_tensor(out=indices[:, 1, :], in0=no_token[:, :], scalar=-1.0, in1=inverse,
                                           op0=ALU.add, op1=ALU.add).then_inc(targets_done, 1)

            dve.wait_ge(expert_w_in, 64)
            dve.wait_ge(indices_done, 1)

            def fetch_w1(i, r):
                e = dve.value_load(tile_expert[0:1, bass.ds(i, 1)], min_val=0, max_val=EXPERTS - 1)
                dve.wait_ge(hidden_done, START + i - 1)
                nc.vector.tensor_copy(w1_now[r][:, :], w1_all[:, bass.ds(e * HIDDEN, HIDDEN)]).then_inc(w1_copied, 1)

            def copy_slotT(i, r):
                dve.wait_ge(slotT_done, i + 1)
                dve.wait_ge(hidden_done, START + i - 1)
                nc.vector.tensor_copy(slotT[r][:, :], bank_s[r][:, 0:P]).then_inc(slotT_copied, 1)

            def finish(i, r, u):
                e = dve.value_load(tile_expert[0:1, bass.ds(i, 1)], min_val=0, max_val=EXPERTS - 1)
                dve.wait_ge(y_done, START + i + 1)
                nc.vector.tensor_tensor(y_bias[r][:, :], bank_o[r][:, 0:D], b2_all[:, bass.ds(e * D, D)], ALU.add
                                        ).then_inc(y_biased, 1)
                dve.wait_ge(y_biased, START + i + 1)
                nc.vector.scalar_tensor_tensor(out=got_rows[u][:, 0:D], in0=y_bias[r][:, :],
                                               scalar=got_rows[u][:, 2 * D:ROW], in1=got_rows[u][:, D:2 * D],
                                               op0=ALU.mult, op1=ALU.add).then_inc(out_done, 1)

            for i in range(2):
                fetch_w1(i, i)
                copy_slotT(i, i)
            for i in range(SLOT_TILES):
                if i + 2 < SLOT_TILES:
                    fetch_w1(i + 2, i % 2)
                    copy_slotT(i + 2, i % 2)
                finish(i, i % 2, i % RING)

        @block.tensor
        def _(pe):
            mm = nc.tensor.matmul
            ident = const("ident")

            def keep_warm(n):
                for _ in range(n):
                    mm(bank_s[0][:, :], warm[:, 0:P], warm[:, :], start=True, stop=True)

            pe.wait_ge(warm_zeroed, 1)
            keep_warm(11)
            pe.wait_ge(consts_in, 16)
            pe.wait_ge(attn_w_in, 16)
            mm(bank_gv[:, 0:P], wat[:, 4, :], const("centre"), start=True, stop=True).then_inc(wv_done, 1)

            def turn(m, r, round_):
                pe.wait_ge(xn_done, m + 1)
                pe.wait_ge(ctx_ld[r], 16 * (round_ + 1))
                pe.wait_ge(xcT_done, m)
                for s, src in enumerate((xn[r], ctx_in[r])):
                    for j in range(2):
                        at = s * UNIT + j * P
                        last = nc.tensor.transpose(bank_t[:, at:at + P], src[:, j, :], ident)
                last.then_inc(xT_done, 1)

            def project_qk(m, r):
                pe.wait_ge(xcT_done, m + 1)
                for bank, w, src, free, done in ((bank_q, 0, 0, q_rotated, q_done), (bank_k, 2, UNIT, k_rotated, k_done)):
                    pe.wait_ge(free, m)
                    for s in range(2):
                        last = mm(bank[:, s * UNIT:s * UNIT + UNIT], wat[:, w + s, :], xcT[r][:, src:src + UNIT],
                                  start=True, stop=True)
                    last.then_inc(done, 1)

            def project_gv(m, r):
                pe.wait_ge(gv_copied, m)
                mm(bank_gv[:, 0:UNIT], wat[:, 5, :], xcT[r][:, 0:UNIT], start=True, stop=True)
                for j in range(2):
                    last = mm(bank_gv[:, UNIT + P * j:UNIT + P * j + P],
                              xcT[r][:, UNIT + P * j:UNIT + P * j + P], w_v[:, :], start=True, stop=True)
                last.then_inc(gv_done, 1)

            def scores(m, r, j):
                if j == 0:
                    pe.wait_ge(qh_done, START + m + 1)
                    pe.wait_ge(kg_done, START + m + 1)
                for gp in range(2):
                    pe.wait_ge(sim_done, START + 4 * m + 2 * j + gp - 1)
                    for b in range(2):
                        for gi in range(2):
                            at = j * P + b * SEQ
                            last = mm(bank_s[gp][SEQ * b:SEQ * b + SEQ, 256 * gi:256 * gi + 256],
                                      k_groups[r][:, 2 * gp + gi, at:at + SEQ],
                                      q_heads[r][:, 2 * j + b, :, :].rearrange("p h i -> p (h i)"),
                                      start=True, stop=True)
                    last.then_inc(scores_done, 1)

            def products(m, r, j):
                tile = 2 * m + j
                if j == 0:
                    pe.wait_ge(gv_copied, m + 1)
                pe.wait_ge(sim_done, START + 4 * m + 2 * j + 2)
                pe.wait_ge(ret_done, START + tile)
                for b in range(2):
                    for g in range(GROUPS):
                        last = mm(bank_o[j][Q * g:Q * g + Q, 256 * b:256 * b + 256],
                                  v_batches[r][:, j, b, Q * g:Q * g + Q],
                                  sim[j][:, g // 2, 256 * (g % 2):256 * (g % 2) + 256], start=True, stop=True)
                last.then_inc(av_done, 1)

            def unit(m, r, next_round, more=True):
                if more:
                    turn(m + 1, 1 - r, next_round)
                scores(m, r, 0)
                if more:
                    project_qk(m + 1, 1 - r)
                products(m, r, 0)
                scores(m, r, 1)
                if more:
                    project_gv(m + 1, 1 - r)
                products(m, r, 1)

            keep_warm(2)
            turn(0, 0, 0)
            project_qk(0, 0)
            pe.wait_ge(wv_copied, 1)
            project_gv(0, 0)
            with pe.Fori(0, (UNITS - 2) // 2) as n:
                unit(2 * n, 0, n)
                unit(2 * n + 1, 1, n + 1)
            unit(UNITS - 2, 0, UNITS // 2 - 1)
            unit(UNITS - 1, 1, 0, more=False)

            pe.wait_ge(late_consts_in, 16)
            pe.wait_ge(xcT_done, UNITS)
            for c in range(4):
                pe.wait_ge(squared, c + 1)
                for h in range(2):
                    at = QUARTER * c + UNIT * h
                    last = mm(bank_t[Q * c:Q * c + Q, 0:UNIT], const("head_mean", 2)[:, h, :], squares[:, at:at + UNIT],
                              start=(h == 0), stop=(h == 1))
            last.then_inc(hvar_done, 1)
            keep_warm(9)

            def spread(c):
                if c >= 2:
                    pe.wait_ge(attn_done, c - 1)
                for h in range(2):
                    last = mm((bank_q, bank_k)[c % 2][:, UNIT * h:UNIT * h + UNIT], const("spread", UNITS)[:, 2 * c + h, :],
                              head_rstd[:, :], start=True, stop=True)
                last.then_inc(spread_done, 1)

            def project_out(c):
                pe.wait_ge(attn_done, c + 1)
                if c >= 2:
                    pe.wait_ge(x1_done, c - 1)
                for t in range(QT):
                    last = mm(bank_o[c % 2][:, P * t:P * t + P], attn[c % 2][:, P * t:P * t + P], wat[:, 6, :],
                              start=True, stop=True)
                last.then_inc(proj_done, 1)

            def turn_xn2(c):
                pe.wait_ge(xn2_done, c + 1)
                if c >= 2:
                    pe.wait_ge(xn2T_copied, c - 1)
                for t in range(QT):
                    last = nc.tensor.transpose(bank_s[c % 2][:, P * t:P * t + P], rows[:, QT * c + t, 0:D], ident)
                last.then_inc(xn2T_done, 1)

            def route(c):
                pe.wait_ge(xn2T_copied, c + 1)
                pe.wait_ge(x1_done, 3)
                for h, bank in enumerate((bank_gv, bank_o[0])):
                    at = QUARTER * c + 2 * P * h
                    last = mm(bank[Q * c:Q * c + Q, 0:2 * P], router_w[:, :], xn2T[:, at:at + 2 * P], start=True, stop=True)
                return last

            pe.wait_ge(bias_in, 64)
            pe.wait_ge(hrstd_done, 1)
            spread(0)
            spread(1)
            for c in range(4):
                project_out(c)
                if c + 2 < 4:
                    spread(c + 2)
                if c >= 2:
                    turn_xn2(c - 2)
                if c >= 3:
                    route(c - 3)
            turn_xn2(2)
            route(1)
            turn_xn2(3)
            route(2)
            route(3).then_inc(logitsT_done, 1)
            pe.wait_ge(logitsT_copied, 2)
            for k in range(QT):
                last = nc.tensor.transpose(bank_t[:, P * k:P * k + P], logitsT[:, P * k:P * k + P], ident)
            last.then_inc(logits_turned, 1)
            pe.wait_ge(chosen_done, 1)
            chosen_cols = chosen[:, :, :].rearrange("p t e -> p (t e)")
            pe.wait_ge(converted, 3)
            mm(bank_q[:, 0:P], before_ones[:, 0, :], chosen_cols, start=True, stop=True)
            mm(bank_k[:, 0:P].rearrange("p (e t) -> p e t", e=EXPERTS), before_ones[:, 1, :],
               chosen[:, :, :].rearrange("p t e -> p e t"), start=True, stop=True).then_inc(ranks_done, 1)
            pe.wait_ge(in_tile_done, 1)
            pe.wait_ge(lanes_done, 1)
            for t in range(TILES):
                last = mm(bank_gv[:, 0:SLOT_TILES], in_lane[:, t, :], in_tile[:, t, :],
                          start=(t == 0), stop=(t == TILES - 1))
            last.then_inc(inverse_done, 1)
            keep_warm(9)

            pe.wait_ge(expert_w_in, 64)
            pe.wait_ge(indices_done, 1)

            def turn_rows(i, r, u, round_):
                pe.wait_ge(got[u], 16 * (round_ + 1))
                pe.wait_ge(slotT_copied, START + i - 1)
                nc.tensor.transpose(bank_s[r][:, 0:P], got_rows[u][:, 0:D], ident).then_inc(slotT_done, 1)

            def first_layer(i, r):
                pe.wait_ge(slotT_copied, START + i + 1)
                pe.wait_ge(w1_copied, i + 1)
                pe.wait_ge(silu_done, START + i - 1)
                for c in range(HC):
                    last = mm((bank_q, bank_k)[r][:, P * c:P * c + P], w1_now[r][:, P * c:P * c + P], slotT[r][:, :],
                              start=True, stop=True)
                last.then_inc(hidden_done, 1)

            def second_layer(i, r):
                e = pe.value_load(tile_expert[0:1, bass.ds(i, 1)], min_val=0, max_val=EXPERTS - 1)
                pe.wait_ge(silu_done, START + i + 1)
                pe.wait_ge(y_biased, START + i - 1)
                for c in range(HC):
                    last = mm(bank_o[r][:, 0:D], hiddenT[r][:, c, :], w2_all[:, bass.ds((e * HC + c) * D, D)],
                              start=(c == 0), stop=(c == HC - 1))
                last.then_inc(y_done, 1)

            turn_rows(0, 0, 0, 0)
            turn_rows(1, 1, 1, 0)
            first_layer(0, 0)
            for i in range(SLOT_TILES):
                if i + 2 < SLOT_TILES:
                    turn_rows(i + 2, i % 2, (i + 2) % RING, (i + 2) // RING)
                if i + 1 < SLOT_TILES:
                    first_layer(i + 1, 1 - i % 2)
                second_layer(i, i % 2)


def constants():
    f = np.float32
    p = np.arange(P)
    head, dim = p // HD, p % HD
    pos = np.arange(SEQ)
    even = np.arange(0, HD, 2, dtype=f)
    length_base = ((even + f(0.4 * HD)) / f(1.4 * HD)).astype(f)
    power = (np.arange(-(SEQ // 2), SEQ - SEQ // 2, dtype=f) / f(512.0))[:, None]
    scale = length_base.astype(np.float64)[None, :] ** power.astype(np.float64)
    half = HD // 2
    inv_freq = (1.0 / 10000.0 ** (np.arange(half, dtype=np.float64) / half)).astype(f)
    angle = (pos.astype(f)[:, None] * inv_freq[None, :]).astype(np.float64)
    sin, cos = np.sin(angle), np.cos(angle)
    gamma = 1.0 - np.exp(np.linspace(np.log(1.0 / 32.0), np.log(1.0 / 512.0), HEADS)).astype(f)
    gamma = gamma.astype(f).astype(np.float64)[head][:, None]
    sign = np.where(dim % 2 == 0, -1.0, 1.0)[:, None]
    pair = dim // 2
    up, down = gamma ** pos[None, :], gamma ** -pos[None, :].astype(np.float64)
    tables = [(cos * scale).T[pair] * up, (sin * scale).T[pair] * up * sign,
              (cos / scale).T[pair] * down, (sin / scale).T[pair] * down * sign]
    quad, lane = p // Q, p % Q
    mean_of_head = np.where(head[:, None] == np.arange(HEADS)[None, :], 1.0 / HD, 0.0)
    nothing = np.zeros((P, HEADS))
    head_mean = np.concatenate([mean_of_head, nothing, nothing, mean_of_head], axis=1)
    spread = np.concatenate([((quad == m // 2) & (lane // HEADS == m % 2))[:, None] *
                             ((lane % HEADS)[:, None] == head[None, :]) for m in range(UNITS)], axis=1)
    full = {
        "ident": np.eye(P),
        "rotary": np.concatenate(tables, axis=1),
        "causal": (p % SEQ)[:, None] <= pos[None, :],
        "head_in_group": (head % GH)[:, None] == np.arange(GH)[None, :],
        "centre": np.eye(P) - (head[:, None] == head[None, :]) / HD,
        "head_mean": head_mean,
        "spread": spread,
        "before": p[:, None] < p[None, :],
        "ones": np.ones((P, P)),
        "iota": np.tile(p, (P, 1)),
        "token_number": P * np.arange(TILES)[None, :] + p[:, None] + 1,
        "expert_rank": np.tile(EXPERTS - np.arange(EXPERTS), (P, 1)),
        "tile_edge": np.tile(P * np.arange(TILES), (P, 1)),
        "not_first_tile": np.tile(np.arange(EXPERTS * TILES) % TILES != 0, (P, 1)),
    }
    out = np.zeros((P, CONST_WIDTH), f)
    for name, _ in CONST_PARTS:
        at, width = CONST_AT[name]
        out[:, at:at + width] = full[name]
    return out


def kernel(x, ctx_1024, L0_xattn_W_Q, L0_xattn_W_K, L0_xattn_W_V, L0_xattn_g_w, L0_xattn_g_b, L0_xattn_out_w,
           L0_xattn_out_b, L0_ffn_Wg, L0_ffn_bg, L0_ffn_W1, L0_ffn_b1, L0_ffn_W2, L0_ffn_b2):
    import concourse.bacc as bacc
    from concourse.bass_utils import run_bass_kernel_spmd

    def per_head(w):
        return np.asarray(w).transpose(1, 0, 2).reshape(D, D)

    swap = np.arange(D) ^ 1
    w_q, w_k, w_v = per_head(L0_xattn_W_Q), per_head(L0_xattn_W_K), per_head(L0_xattn_W_V)
    stacked = [w_q, w_q[:, swap], w_k, w_k[:, swap], w_v.T, np.asarray(L0_xattn_g_w).T, np.asarray(L0_xattn_out_w).T]
    router = np.zeros((D, Q), np.float32)
    router[:, :EXPERTS] = np.asarray(L0_ffn_Wg)
    router_bias = np.zeros((4, Q), np.float32)
    router_bias[:, :EXPERTS] = np.asarray(L0_ffn_bg)
    arrays = {
        "x": np.asarray(x).reshape(TOKENS, D),
        "ctx": np.asarray(ctx_1024).reshape(TOKENS, D),
        "w_attn": np.stack(stacked, axis=1),
        "g_b": np.asarray(L0_xattn_g_b).reshape(D, 1),
        "out_b": np.asarray(L0_xattn_out_b),
        "w_gate": router,
        "b_gate": router_bias.reshape(P, 1),
        "w1": np.asarray(L0_ffn_W1).transpose(1, 0, 2).reshape(D, EXPERTS * HIDDEN),
        "b1": np.asarray(L0_ffn_b1).reshape(EXPERTS * HC, P).T,
        "w2": np.asarray(L0_ffn_W2).reshape(EXPERTS, HC, P, D).transpose(2, 0, 1, 3).reshape(P, EXPERTS * HC * D),
        "b2": np.asarray(L0_ffn_b2).reshape(EXPERTS * D),
        "consts": constants(),
    }
    nc = bacc.Bacc("TRN2", target_bir_lowering=False, num_devices=1)
    args, ins = [], {}
    for name, a in arrays.items():
        ins[f"in_{name}"] = np.ascontiguousarray(a)
        args.append(nc.dram_tensor(f"in_{name}", a.shape, mybir.dt.from_np(a.dtype), kind="ExternalInput").ap())
    out = nc.dram_tensor("out", (TOKENS, D), F32, kind="ExternalOutput").ap()
    build(nc, *args, out)
    result = run_bass_kernel_spmd(nc, [ins], core_ids=[0])
    return result.results[0]["out"].reshape(BATCH, SEQ, D)
```

```python
from contextlib import ExitStack

import numpy as np
import concourse.bass as bass
from concourse import mybir

F32 = mybir.dt.float32
BF16 = mybir.dt.bfloat16
F16 = mybir.dt.float16
I32 = mybir.dt.int32
ALU = mybir.AluOpType
ACT = mybir.ActivationFunctionType
AX = mybir.AxisListType

P = 128
BATCH, SEQ, D = 32, 64, 128
HEADS, HD = 16, 8
TOKENS = BATCH * SEQ
TILES = TOKENS // P
UNIT = 2 * P
UNITS = TOKENS // UNIT
EARLY = 3
UB = UNIT // SEQ
GROUPS = 4
GH = HEADS // GROUPS
HH = HEADS // 2
HK = SEQ // 2
Q = 32
QUARTER = TOKENS // 4
QT = TILES // 4
EXPERTS, HIDDEN = 8, 512
HC = HIDDEN // P
SLOT_TILES = TILES + EXPERTS - 1
ROW = 2 * D + 1
EPS = 1e-5
FIRST_PLANES = 4
ACT_PLANES = 6
RING = 12
NO_TOKEN = 1 << 16

CONST_PARTS = [("ident", P), ("rotary_q", 2 * SEQ), ("rotary_k", 2 * P), ("causal", 2 * SEQ),
               ("head_in_group", GH), ("head_in_half", HH), ("batch_of_key", 2),
               ("centre", P), ("eps", 1), ("head_mean", 2 * Q), ("spread", UNITS * P), ("before", P), ("ones", P),
               ("iota", P), ("token_number", TILES), ("expert_rank", EXPERTS),
               ("tile_edge", TILES), ("not_first_tile", EXPERTS * TILES)]
CONST_AT, _at = {}, 0
for _name, _width in CONST_PARTS:
    CONST_AT[_name] = (_at, _width)
    _at += _width
CONST_WIDTH = _at
EARLY_CONSTS = CONST_AT["head_mean"][0]
ATTN_WEIGHTS = ["q", "q_pair_swapped", "k", "k_pair_swapped", "v_transposed", "gate", "out"]


def build(nc, x, ctx, w_attn, g_b, out_b, w_gate, b_gate, w1, b1, w2, b2, consts, out):
    stack = ExitStack()
    with stack:
        def sb(name, shape, dt=F32):
            return stack.enter_context(nc.sbuf_tensor(name, shape, dt))

        def bank(name):
            return stack.enter_context(nc.psum_tensor(name, [P, 512], F32))

        def sem(name):
            return stack.enter_context(nc.semaphore(name))

        token_rows = nc.dram_tensor("token_rows", [TOKENS, ROW], F32, kind="Internal").ap()

        cst = sb("cst", [P, CONST_WIDTH])
        wat = sb("wat", [P, len(ATTN_WEIGHTS), P])
        w_v = sb("w_v", [P, P])
        warm = sb("warm", [P, 512], BF16)
        unused = sb("unused", [P, 4])
        gate_bias = sb("gate_bias", [P, 1])
        out_bias = sb("out_bias", [P, D])
        router_bias = sb("router_bias", [P, 1])
        router_w = sb("router_w", [P, Q])
        w1_all = sb("w1_all", [P, EXPERTS * HIDDEN])
        w2_all = sb("w2_all", [P, EXPERTS * HC * D])
        b1_all = sb("b1_all", [P, EXPERTS * HC])
        b2_all = sb("b2_all", [P, EXPERTS * D])
        x_all = sb("x_all", [P, TILES, D])
        x_plus_b = sb("x_plus_b", [P, TILES, D])
        stats = sb("stats", [P, TILES, 6])
        mean_var = sb("mean_var", [P, TILES, 2])
        std = sb("std", [P, TILES])
        rstd = sb("rstd", [P, TILES])
        xn = [sb(f"xn{r}", [P, 2, D]) for r in range(2)]
        ctx_in = [sb(f"ctx_in{r}", [P, 2, D]) for r in range(2)]
        xcT = [sb(f"xcT{r}", [P, 2 * UNIT]) for r in range(2)]
        q_parts = sb("q_parts", [P, 2, UNIT])
        k_parts = sb("k_parts", [P, 2, UNIT])
        q_sum = [sb(f"q_sum{r}", [P, UNIT]) for r in range(2)]
        k_sum = [sb(f"k_sum{r}", [P, UNIT]) for r in range(2)]
        q_heads = [sb(f"q_heads{r}", [P, UB, HH, SEQ]) for r in range(2)]
        k_halves = [sb(f"k_halves{r}", [P, 2, UNIT]) for r in range(2)]
        v_batches = [sb(f"v_batches{r}", [P, 2, 2, P]) for r in range(2)]
        sim = [sb(f"sim{j}", [P, 2, 512]) for j in range(2)]
        ret_sum = [sb(f"ret_sum{j}", [P, GH - 1, P]) for j in range(2)]
        retT = sb("retT", [P, TOKENS])
        gateT = sb("gateT", [P, TOKENS])
        ret_gate = sb("ret_gate", [P, TOKENS])
        squares = x_all[:, :, :].rearrange("p t d -> p (t d)")
        head_std = sb("head_std", [P, UNIT])
        head_rstd = [sb(f"head_rstd{k}", [P, UNIT]) for k in range(2)]
        attn = [sb(f"attn{r}", [P, QUARTER]) for r in range(2)]
        rows = sb("rows", [P, TILES, 2 * D])
        stats2 = sb("stats2", [P, TILES, 6])
        mean_var2 = sb("mean_var2", [P, TILES, 2])
        std2 = sb("std2", [P, TILES])
        rstd2 = sb("rstd2", [P, TILES])
        shift2 = sb("shift2", [P, TILES])
        xn2T = retT
        logitsT = sb("logitsT", [P, 512])
        te = [P, TILES, EXPERTS]
        top = sb("top", [P, TILES])
        below_top = sb("below_top", te)
        powers = sb("powers", te)
        power_sum = sb("power_sum", [P, TILES])
        top_weight = sb("top_weight", [P, TILES])
        rank_of_top = sb("rank_of_top", te)
        best_rank = sb("best_rank", [P, TILES])
        chosen = sb("chosen", te, BF16)
        counts_to = sb("counts_to", [P, EXPERTS, TILES])
        tiles_used = sb("tiles_used", [P, EXPERTS, TILES])
        n_tiles = sb("n_tiles", [P, EXPERTS])
        end_tile = sb("end_tile", [P, EXPERTS])
        base = sb("base", [P, EXPERTS])
        counts_before = sb("counts_before", [P, EXPERTS, TILES])
        place = sb("place", te)
        base_chosen = sb("base_chosen", te)
        place_chosen = sb("place_chosen", te)
        first_tile = sb("first_tile", [P, TILES])
        rank = sb("rank", [P, TILES])
        rank_i = sb("rank_i", [P, TILES], I32)
        rank_parts = sb("rank_parts", [P, 2, TILES], I32)
        slot_parts = sb("slot_parts", [P, 2, TILES], F16)
        past_end = sb("past_end", [P, SLOT_TILES, EXPERTS])
        tile_expert_f = sb("tile_expert_f", [P, SLOT_TILES])
        tile_expert = sb("tile_expert", [P, SLOT_TILES], I32)
        is_tile = sb("is_tile", [P, TILES, SLOT_TILES], F16)
        in_tile = sb("in_tile", [P, TILES, SLOT_TILES], F16)
        in_lane = sb("in_lane", [P, TILES, P], F16)
        iota_h = sb("iota_h", [P, P], F16)
        before_ones = sb("before_ones", [P, 2, P], BF16)
        no_token = sb("no_token", [P, SLOT_TILES])
        indices = sb("indices", [P, 2, SLOT_TILES], I32)
        got_rows = [sb(f"got_rows{u}", [P, ROW]) for u in range(RING)]
        slotT = [sb(f"slotT{r}", [P, P]) for r in range(2)]
        w1_now = [sb(f"w1_now{r}", [P, HIDDEN]) for r in range(2)]
        hiddenT = [sb(f"hiddenT{r}", [P, HC, P]) for r in range(2)]
        y_bias = [sb(f"y_bias{r}", [P, D]) for r in range(2)]

        bank_t, bank_q, bank_k, bank_gv = (bank(f"bank_{n}") for n in ("t", "q", "k", "gv"))
        bank_s = [bank(f"bank_s{i}") for i in range(2)]
        bank_o = [bank(f"bank_o{i}") for i in range(2)]
        proj_banks = [bank_gv, bank_s[0]]
        turn2_banks = [bank_s[1], bank_o[0]]
        logit_banks = [bank_t, bank_o[1]]

        def const(name, *dims):
            at, width = CONST_AT[name]
            part = cst[:, at:at + width]
            if dims:
                part = part.rearrange("p (a b) -> p a b", a=dims[0])
            return part

        consts_in, late_consts_in, attn_w_in, bias_in, expert_w_in = map(
            sem, ("consts_in", "late_consts_in", "attn_w_in", "bias_in", "expert_w_in"))
        x_in = [sem(f"x_in{c}") for c in range(4)]
        ctx_ld = [sem(f"ctx_ld{r}") for r in range(2)]
        zeroed, warm_zeroed, head_zeroed, sim_zeroed = map(sem, ("zeroed", "warm_zeroed", "head_zeroed", "sim_zeroed"))
        xb_done = sem("xb_done")
        dve_step = sem("dve_step")
        var_done, std_done, rstd_done = map(sem, ("var_done", "std_done", "rstd_done"))
        all_stats_done, first_qh_done = map(sem, ("all_stats_done", "first_qh_done"))
        wv_done, wv_copied = map(sem, ("wv_done", "wv_copied"))
        xn_done, xT_done, xcT_done = map(sem, ("xn_done", "xT_done", "xcT_done"))
        q_done, k_done, gv_done = map(sem, ("q_done", "k_done", "gv_done"))
        q_rotated, k_rotated, q_summed, k_summed = map(sem, ("q_rotated", "k_rotated", "q_summed", "k_summed"))
        qh_done, last_qh_done, kh_done, gv_copied = map(sem, ("qh_done", "last_qh_done", "kh_done", "gv_copied"))
        scores_done, sim_done, av_done = map(sem, ("scores_done", "sim_done", "av_done"))
        head0_done, head_added, ret_done = map(sem, ("head0_done", "head_added", "ret_done"))
        squared, ret_gated, hvar_done, hstd_done, hrstd_done = map(
            sem, ("squared", "ret_gated", "hvar_done", "hstd_done", "hrstd_done"))
        spread_done, attn_done, proj_done, x1_done = map(sem, ("spread_done", "attn_done", "proj_done", "x1_done"))
        (var2_done, std2_done, rstd2_done, xn2_done, last_xn2_done, xn2T_done, xn2T_copied, last_xn2T_done,
         last_xn2T_copied) = map(
            sem, ("var2_done", "std2_done", "rstd2_done", "xn2_done", "last_xn2_done", "xn2T_done", "xn2T_copied",
                  "last_xn2T_done", "last_xn2T_copied"))
        logitsT_done, logitsT_copied, logits_turned = map(sem, ("logitsT_done", "logitsT_copied", "logits_turned"))
        below_done, powers_done, weight_done = map(sem, ("below_done", "powers_done", "weight_done"))
        converted, chosen_done, ranks_done, slots_done, lanes_done = map(
            sem, ("converted", "chosen_done", "ranks_done", "slots_done", "lanes_done"))
        is_tile_done, in_tile_done, inverse_done, indices_done, experts_known, targets_done = map(
            sem, ("is_tile_done", "in_tile_done", "inverse_done", "indices_done",
                  "experts_known", "targets_done"))
        rows_out, weights_out = map(sem, ("rows_out", "weights_out"))
        got = [sem(f"got{u}") for u in range(RING)]
        scattered = [sem(f"scattered{u}") for u in range(RING)]
        slotT_done, slotT_copied, w1_copied = map(sem, ("slotT_done", "slotT_copied", "w1_copied"))
        hidden_done, silu_done, y_done, y_biased, out_done = map(
            sem, ("hidden_done", "silu_done", "y_done", "y_biased", "out_done"))

        START = 4 + 1
        ring_counts = [xT_done, gv_done, scores_done, av_done, ret_done, sim_done, kh_done, qh_done, last_qh_done,
                       slotT_copied, hidden_done, silu_done, y_done, y_biased]

        block = stack.enter_context(nc.Block())

        @block.sync
        def _(sp):
            x_tiles = x.rearrange("(t p) d -> p t d", p=P)
            ctx_units = ctx.rearrange("(m j p) d -> m p j d", p=P, j=2)

            def load_ctx(m, r):
                sp.wait_ge(xT_done, START + m - 1)
                sp.dma_start(ctx_in[r][:, :, :],
                             ctx_units[m] if isinstance(m, int)
                             else ctx_units[bass.ds(m, 1)].rearrange("m p j d -> (m p) j d")
                             ).then_inc(ctx_ld[r], 16)

            for c in range(4):
                sp.dma_start(x_all[:, QT * c:QT * c + QT, :], x_tiles[:, QT * c:QT * c + QT, :]).then_inc(x_in[c], 16)
                if c == 0:
                    load_ctx(0, 0)
                    sp.dma_start(wat[:, :, :], w_attn).then_inc(attn_w_in, 16)
            load_ctx(1, 1)
            sp.dma_start(out_bias[:, :], out_b.partition_broadcast(P)).then_inc(bias_in, 16)
            sp.dma_start(router_bias[:, :], b_gate).then_inc(bias_in, 16)
            sp.dma_start(router_w[:, :], w_gate).then_inc(bias_in, 16)
            sp.dma_start(cst[:, EARLY_CONSTS:CONST_WIDTH], consts[:, EARLY_CONSTS:CONST_WIDTH]).then_inc(late_consts_in, 16)
            for m in range(2, UNITS):
                load_ctx(m, m % 2)
            sp.dma_start(w1_all[:, :], w1).then_inc(expert_w_in, 16)
            sp.dma_start(w2_all[:, :], w2).then_inc(expert_w_in, 16)
            sp.dma_start(b1_all[:, :], b1).then_inc(expert_w_in, 16)
            sp.dma_start(b2_all[:, :], b2.partition_broadcast(P)).then_inc(expert_w_in, 16)
            row_tiles = token_rows.rearrange("(t p) r -> p t r", p=P)
            for c in range(4):
                if c < EARLY:
                    sp.wait_ge(xn2_done, c + 1)
                else:
                    sp.wait_ge(last_xn2_done, 1)
                sp.dma_start(row_tiles[:, QT * c:QT * c + QT, 0:2 * D], rows[:, QT * c:QT * c + QT, :]
                             ).then_inc(rows_out, 16)
            sp.wait_ge(weight_done, 1)
            with nc.allow_non_contiguous_dma(reason="one weight per token"):
                sp.dma_start(row_tiles[:, :, 2 * D:ROW], top_weight[:, :].unsqueeze(2)).then_inc(weights_out, 16)

        @block.gpsimd
        def _(pool):
            for count in ring_counts:
                pool.sem_inc(count, START)
            for r in range(2):
                pool.memset(k_halves[r][:, :, :], 0.0).then_inc(zeroed, 1)
            for k in range(2):
                pool.memset(head_rstd[k][:, :], 0.0).then_inc(head_zeroed, 1)

            def add_k(m, r):
                pool.wait_ge(k_rotated, m + 1)
                pool.wait_ge(kh_done, START + m - 1)
                pool.tensor_tensor(k_sum[r][:, :], k_parts[:, 0, :], k_parts[:, 1, :], ALU.add).then_inc(k_summed, 1)

            def split_q(m, r):
                pool.wait_ge(q_summed, m + 1)
                pool.wait_ge(scores_done, START + 4 * (m - 1))
                for h in range(ACT_PLANES, HH):
                    last = pool.tensor_tensor(q_heads[r][:, :, h, :], q_sum[r][:, :].rearrange("p (b i) -> p b i", b=UB),
                                              const("head_in_half")[:, h:h + 1].unsqueeze(2).broadcast_to([P, UB, SEQ]),
                                              ALU.mult)
                last.then_inc(last_qh_done, 1)

            pool.wait_ge(consts_in, 16)
            add_k(0, 0)
            split_q(0, 0)
            pool.wait_ge(bias_in, 64)
            for c in range(4):
                pool.wait_ge(x_in[c], 16)
                tiles = slice(QT * c, QT * c + QT)
                pool.tensor_tensor(x_plus_b[:, tiles, :], x_all[:, tiles, :],
                                   out_bias[:, :].unsqueeze(1).broadcast_to([P, QT, D]), ALU.add).then_inc(xb_done, 1)
                if c == 0:
                    add_k(1, 1)
                    split_q(1, 1)
            with pool.Fori(0, (UNITS - 2) // 2) as n:
                for r in range(2):
                    add_k(2 * n + 2 + r, r)
                    split_q(2 * n + 2 + r, r)
            for c in range(4):
                cols = slice(QUARTER * c, QUARTER * c + QUARTER)
                pool.wait_ge(ret_done, START + QT * (c + 1))
                pool.wait_ge(gv_copied, 2 * (c + 1))
                pool.tensor_tensor(ret_gate[:, cols], retT[:, cols], gateT[:, cols], ALU.mult).then_inc(ret_gated, 1)

            ts = [P, TILES, SLOT_TILES]
            pool.wait_ge(late_consts_in, 16)
            pool.wait_ge(is_tile_done, 1)
            pool.tensor_tensor(in_tile[:, :, :], is_tile[:, :, :], const("token_number").unsqueeze(2).broadcast_to(ts),
                               ALU.mult).then_inc(in_tile_done, 1)

            last_row = pool.to_reg(TOKENS - 1)
            pool.wait_ge(indices_done, 1)
            pool.wait_ge(rows_out, 64)
            pool.wait_ge(weights_out, 16)


            def gather(i):
                u = i % RING
                if i >= RING:
                    pool.wait_ge(scattered[u], 16 * (i // RING))
                pool.indirect_dma_start(out=got_rows[u][:, :], out_offset=None, in_=token_rows[:, :],
                                        in_offset=bass.IndirectOffsetOnAxis(ap=indices[:, 0, i:i + 1], axis=0),
                                        bounds_check=last_row, oob_is_err=False).then_inc(got[u], 16)

            def scatter(i):
                pool.wait_ge(out_done, i + 1)
                if i == 0:
                    pool.wait_ge(targets_done, 1)
                pool.indirect_dma_start(out=out[:, :],
                                        out_offset=bass.IndirectOffsetOnAxis(ap=indices[:, 1, i:i + 1], axis=0),
                                        in_=got_rows[i % RING][:, 0:D], in_offset=None,
                                        bounds_check=last_row, oob_is_err=False).then_inc(scattered[i % RING], 16)

            AHEAD = RING - 2
            for i in range(AHEAD):
                gather(i)
            for i in range(SLOT_TILES):
                if i + AHEAD < SLOT_TILES:
                    gather(i + AHEAD)
                scatter(i)
            for u in range(RING):
                pool.wait_ge(scattered[u], 16 * len(range(u, SLOT_TILES, RING)))

        @block.scalar
        def _(act):
            act.dma_start(cst[:, 0:EARLY_CONSTS], consts[:, 0:EARLY_CONSTS]).then_inc(consts_in, 16)
            act.wait_ge(warm_zeroed, 1)
            nc.scalar.activation(unused[:, 0:1], warm[:, 0:1], ACT.Sqrt)
            act.dma_start(gate_bias[:, :], g_b).then_inc(bias_in, 16)
            def roots(tiles, step):
                act.wait_ge(var_done, step)
                nc.scalar.activation(std[:, tiles], mean_var[:, tiles, 1], ACT.Sqrt, bias=const("eps")).then_inc(std_done, 1)

            act.wait_ge(consts_in, 16)
            roots(slice(0, QT), 1)
            act.wait_ge(wv_done, 1)
            nc.scalar.activation(w_v[:, :], bank_gv[:, 0:P], ACT.Copy).then_inc(wv_copied, 1)
            head_mask = const("head_in_group")

            def copy_transposed(m, r):
                act.wait_ge(xT_done, START + m + 1)
                act.wait_ge(gv_done, START + m - 1)
                nc.scalar.activation(xcT[r][:, :], bank_t[:, :], ACT.Copy).then_inc(xcT_done, 1)

            def split_q(m, r, planes=ACT_PLANES):
                act.wait_ge(q_summed, m + 1)
                act.wait_ge(scores_done, START + 4 * (m - 1))
                for h in range(planes):
                    last = nc.scalar.activation(q_heads[r][:, :, h, :], q_sum[r][:, :].rearrange("p (b i) -> p b i", b=UB),
                                                ACT.Copy, scale=const("head_in_half")[:, h:h + 1])
                last.then_inc(qh_done, 1)

            def split_k(m, r):
                act.wait_ge(k_summed, m + 1)
                act.wait_ge(scores_done, START + 4 * (m - 1))
                for half in range(2):
                    rows_of = slice(HH * HD * half, HH * HD * (half + 1))
                    last = nc.scalar.activation(k_halves[r][rows_of, half, :], k_sum[r][rows_of, :], ACT.Copy)
                last.then_inc(kh_done, 1)

            def gate_and_values(m, r):
                act.wait_ge(gv_done, START + m + 1)
                act.wait_ge(av_done, START + 2 * (m - 1))
                nc.scalar.activation(gateT[:, bass.ds(m * UNIT, UNIT)], bank_gv[:, 0:UNIT], ACT.Silu,
                                     bias=gate_bias[:, 0:1])
                values = bank_gv[:, UNIT:2 * UNIT].rearrange("p (j f) -> p j f", j=2)
                for b in range(2):
                    ours = const("batch_of_key")[:, b:b + 1]
                    for to, frm, half in ((slice(0, P), slice(0, P), 0), (slice(0, 64), slice(64, P), 1),
                                          (slice(64, P), slice(0, 64), 1)):
                        f = slice(64 * half, 64 * half + 64)
                        last = nc.scalar.activation(v_batches[r][to, :, b, f], values[frm, :, f], ACT.Copy,
                                                    scale=ours[frm])
                last.then_inc(gv_copied, 1)

            def first_head(m, j):
                tile = 2 * m + j
                act.wait_ge(av_done, START + tile + 1)
                act.wait_ge(ret_done, START + tile - 1)
                nc.scalar.activation(ret_sum[j][:, 0, :].rearrange("p (b i) -> p b i", b=2),
                                     bank_o[j][:, :].rearrange("p (b h i) -> p b h i", b=2, h=GH)[:, :, 0, :],
                                     ACT.Copy, scale=head_mask[:, 0:1]).then_inc(head0_done, 1)

            def unit(m, r):
                first_head(m, 0)
                split_q(m + 1, 1 - r)
                split_k(m + 1, 1 - r)
                first_head(m, 1)
                copy_transposed(m + 2, r)
                gate_and_values(m + 1, 1 - r)

            copy_transposed(0, 0)
            act.wait_ge(bias_in, 64)
            act.wait_ge(zeroed, 2)
            split_q(0, 0, FIRST_PLANES)
            roots(slice(QT, TILES), 2)
            copy_transposed(1, 1)
            gate_and_values(0, 0)
            with act.Fori(0, (UNITS - 2) // 2) as n:
                for r in range(2):
                    unit(2 * n + r, r)

            def square(c):
                cols = slice(QUARTER * c, QUARTER * c + QUARTER)
                act.wait_ge(ret_done, START + QT * (c + 1))
                act.wait_ge(xb_done, c + 1)
                nc.scalar.activation(squares[:, cols], retT[:, cols], ACT.Square).then_inc(squared, 1)

            def head_roots(k, bank, lanes):
                act.wait_ge(hvar_done, k + 1)
                nc.scalar.activation(head_std[lanes, :], bank[lanes, 0:UNIT], ACT.Sqrt, bias=const("eps")[lanes]
                                     ).then_inc(hstd_done, 1)

            last = UNITS - 1
            act.wait_ge(xn_done, UNITS)
            for c in range(EARLY):
                square(c)
            first_head(last - 1, 0)
            split_q(last, 1)
            split_k(last, 1)
            first_head(last - 1, 1)
            gate_and_values(last, 1)
            head_roots(0, bank_t, slice(0, Q * EARLY))
            first_head(last, 0)
            act.wait_ge(late_consts_in, 16)
            nc.scalar.activation(before_ones[:, 0, :], const("before"), ACT.Copy).then_inc(converted, 1)
            nc.scalar.activation(before_ones[:, 1, :], const("ones"), ACT.Copy).then_inc(converted, 1)
            nc.scalar.activation(iota_h[:, :], const("iota"), ACT.Copy).then_inc(converted, 1)
            first_head(last, 1)

            def copy_x1(c):
                act.wait_ge(proj_done, c + 1)
                nc.scalar.activation(rows[:, QT * c:QT * c + QT, D:2 * D],
                                     proj_banks[c % 2][:, :].rearrange("p (t d) -> p t d", d=D), ACT.Copy
                                     ).then_inc(x1_done, 1)

            copy_x1(0)
            square(EARLY)
            head_roots(1, bank_t, slice(Q * EARLY, P))

            def copy_xn2T(c):
                act.wait_ge(xn2T_done, c + 1)
                nc.scalar.activation(xn2T[:, QUARTER * c:QUARTER * c + QUARTER], turn2_banks[c % 2][:, :], ACT.Copy
                                     ).then_inc(xn2T_copied, 1)

            def roots2(c):
                act.wait_ge(var2_done, c + 1)
                nc.scalar.activation(std2[:, QT * c:QT * c + QT], mean_var2[:, QT * c:QT * c + QT, 1], ACT.Sqrt,
                                     bias=const("eps")).then_inc(std2_done, 1)

            def normalise2(c):
                act.wait_ge(rstd2_done, c + 1)
                for t in range(QT * c, QT * c + QT):
                    last = nc.scalar.activation(rows[:, t, 0:D], rows[:, t, D:2 * D], ACT.Identity,
                                                bias=shift2[:, t:t + 1], scale=rstd2[:, t:t + 1])
                last.then_inc(xn2_done, 1)

            roots2(0)
            copy_x1(1)
            normalise2(0)
            roots2(1)
            copy_x1(2)
            copy_x1(3)
            normalise2(1)
            roots2(2)
            roots2(3)
            copy_xn2T(0)
            copy_xn2T(1)
            normalise2(2)
            copy_xn2T(2)
            act.wait_ge(logitsT_done, 1)
            nc.scalar.activation(logitsT[:, 0:2 * P], logit_banks[0][:, 0:2 * P], ACT.Identity, bias=router_bias[:, 0:1]
                                 ).then_inc(logitsT_copied, 1)
            act.wait_ge(below_done, 1)
            nc.scalar.activation(powers[:, :, :], below_top[:, :, :], ACT.Exp).then_inc(powers_done, 1)
            nc.scalar.activation(unused[:, 2:3], warm[:, 0:1], ACT.Silu)

            act.wait_ge(expert_w_in, 64)
            act.wait_ge(experts_known, 1)

            def silu(i, r):
                e = act.value_load(tile_expert[0:1, bass.ds(i, 1)], min_val=0, max_val=EXPERTS - 1)
                act.wait_ge(hidden_done, START + i + 1)
                act.wait_ge(y_done, START + i - 1)
                h_bank = (bank_q, bank_k)[r]
                for c in range(HC):
                    last = nc.scalar.activation(hiddenT[r][:, c, :], h_bank[:, P * c:P * c + P], ACT.Silu,
                                                bias=b1_all[:, bass.ds(e * HC + c, 1)])
                last.then_inc(silu_done, 1)

            for i in range(SLOT_TILES):
                silu(i, i % 2)

        @block.vector
        def _(dve):
            steps = [0]

            def step(ins):
                steps[0] += 1
                ins.then_inc(dve_step, 1)
                return steps[0]

            def chain(ins):
                dve.wait_ge(dve_step, step(ins))

            nc.vector.memset(warm[:, :], 0.0).then_inc(warm_zeroed, 1)
            for j in range(2):
                for half, lanes in ((0, slice(64, P)), (1, slice(0, 64))):
                    nc.vector.memset(sim[j][lanes, half, :].rearrange("p (h i) -> p h i", i=SEQ)[:, :, 0:HK], 0.0
                                     ).then_inc(sim_zeroed, 1)

            def statistics(first, end):
                for t in range(first, end):
                    if t % QT == 0:
                        dve.wait_ge(x_in[t // QT], 16)
                    last = nc.vector.bn_stats(stats[:, t, :], x_all[:, t, :])
                return last

            def variances(first, end):
                for t in range(first, end):
                    last = nc.vector.bn_aggr(mean_var[:, t, :], stats[:, t, :])
                last.then_inc(var_done, 1)

            def invert_std(first, end, step):
                dve.wait_ge(std_done, step)
                nc.vector.reciprocal(rstd[:, first:end], std[:, first:end]).then_inc(rstd_done, 1)
                dve.wait_ge(rstd_done, step)

            chain(statistics(0, QT))
            variances(0, QT)
            invert_std(0, QT, 1)

            rotary_q = const("rotary_q", 2).unsqueeze(2).broadcast_to([P, 2, UB, SEQ])
            rotary_k = const("rotary_k", 2).unsqueeze(2).broadcast_to([P, 2, 2, P])
            causal = const("causal", 2)
            head_mask = const("head_in_group")

            def normalise(m, r):
                dve.wait_ge(xT_done, START + m - 1)
                for j in range(2):
                    tile = 2 * m + j
                    last = nc.vector.tensor_scalar(
                        xn[r][:, j, :], x_all[:, bass.ds(tile, 1), :].rearrange("p a d -> p (a d)"),
                        mean_var[:, bass.ds(tile, 1), 0:1].rearrange("p a b -> p (a b)"),
                        rstd[:, bass.ds(tile, 1)], ALU.subtract, ALU.mult)
                last.then_inc(xn_done, 1)

            def rotate(parts, bank, table):
                n = table.shape[2]
                return nc.vector.tensor_tensor(
                    parts[:, :, :].rearrange("p s (b i) -> p s b i", b=n),
                    bank[:, :].rearrange("p (s b i) -> p s b i", s=2, b=n), table, ALU.mult)

            def rotate_qk(m, r):
                dve.wait_ge(q_done, m + 1)
                dve.wait_ge(q_summed, m)
                rotate(q_parts, bank_q, rotary_q).then_inc(q_rotated, 1)
                dve.wait_ge(k_done, m + 1)
                dve.wait_ge(k_summed, m)
                rotate(k_parts, bank_k, rotary_k).then_inc(k_rotated, 1)
                dve.wait_ge(q_rotated, m + 1)
                dve.wait_ge(qh_done, START + m - 1)
                dve.wait_ge(last_qh_done, START + m - 1)
                nc.vector.tensor_tensor(q_sum[r][:, :], q_parts[:, 0, :], q_parts[:, 1, :], ALU.add
                                        ).then_inc(q_summed, 1)

            def mask_scores(m, j):
                tile = 2 * m + j
                for gp in range(2):
                    dve.wait_ge(scores_done, START + 4 * m + 2 * j + gp + 1)
                    if gp == 0:
                        dve.wait_ge(av_done, START + tile - 1)
                    first_block = slice(64 * gp, 64 * gp + 64)
                    for lanes, queries in ((first_block, slice(0, HK)), (slice(0, P), slice(HK, SEQ))):
                        n = lanes.stop - lanes.start
                        last = nc.vector.tensor_tensor(
                            sim[j][lanes, gp, :].rearrange("p (h i) -> p h i", i=SEQ)[:, :, queries],
                            bank_s[gp][lanes, :].rearrange("p (h i) -> p h i", i=SEQ)[:, :, queries],
                            causal[lanes, gp, queries].unsqueeze(1).broadcast_to([n, HH, HK]), ALU.mult)
                    last.then_inc(sim_done, 1)

            def add_heads(m, j):
                tile = 2 * m + j
                products = bank_o[j][:, :].rearrange("p (b h i) -> p b h i", b=2, h=GH)
                dve.wait_ge(head0_done, tile + 1)
                for h in range(1, GH):
                    if h > 1:
                        dve.wait_ge(head_added, 2 * tile + h - 1)
                    before = ret_sum[j][:, h - 1, :].rearrange("p (b i) -> p b i", b=2)
                    after = ret_sum[j][:, h, :] if h < GH - 1 else retT[:, bass.ds(tile * P, P)]
                    ins = nc.vector.scalar_tensor_tensor(
                        out=after.rearrange("p (b i) -> p b i", b=2), in0=products[:, :, h, :],
                        scalar=head_mask[:, h:h + 1], in1=before, op0=ALU.mult, op1=ALU.add)
                    ins.then_inc(head_added if h < GH - 1 else ret_done, 1)

            def unit(m, r):
                mask_scores(m, 0)
                rotate_qk(m + 1, 1 - r)
                normalise(m + 2, r)
                mask_scores(m, 1)
                add_heads(m, 0)
                add_heads(m, 1)

            normalise(0, 0)
            normalise(1, 1)
            statistics(QT, TILES).then_inc(all_stats_done, 1)
            dve.wait_ge(consts_in, 16)
            rotate_qk(0, 0)
            dve.wait_ge(q_summed, 1)
            for h in range(FIRST_PLANES, ACT_PLANES):
                last = nc.vector.tensor_scalar(q_heads[0][:, :, h, :], q_sum[0][:, :].rearrange("p (b i) -> p b i", b=UB),
                                               const("head_in_half")[:, h:h + 1], None, ALU.mult)
            last.then_inc(first_qh_done, 1)
            dve.wait_ge(k_summed, 1)
            dve.wait_ge(zeroed, 2)
            for half in range(2):
                rows_of = slice(HH * HD * half, HH * HD * (half + 1))
                last = nc.vector.tensor_copy(k_halves[0][rows_of, half, :], k_sum[0][rows_of, :])
            last.then_inc(kh_done, 1)
            dve.wait_ge(all_stats_done, 1)
            variances(QT, TILES)
            invert_std(QT, TILES, 2)
            with dve.Fori(0, (UNITS - 2) // 2) as n:
                for r in range(2):
                    unit(2 * n + r, r)

            def invert_heads(k, lanes):
                dve.wait_ge(hstd_done, k + 1)
                return nc.vector.reciprocal(head_rstd[k][lanes, :], head_std[lanes, :])

            def close_attention(c):
                dve.wait_ge(spread_done, c + 1)
                dve.wait_ge(ret_gated, c + 1)
                if c >= 2:
                    dve.wait_ge(proj_done, c - 1)
                nc.vector.tensor_tensor(attn[c % 2][:, :], (bank_q, bank_k)[c % 2][:, :],
                                        ret_gate[:, QUARTER * c:QUARTER * c + QUARTER], ALU.mult
                                        ).then_inc(attn_done, 1)

            def statistics2(c):
                dve.wait_ge(x1_done, c + 1)
                for t in range(QT * c, QT * c + QT):
                    last = nc.vector.bn_stats(stats2[:, t, :], rows[:, t, D:2 * D])
                chain(last)
                for t in range(QT * c, QT * c + QT):
                    last = nc.vector.bn_aggr(mean_var2[:, t, :], stats2[:, t, :])
                last.then_inc(var2_done, 1)

            def invert_std2(c):
                tiles = slice(QT * c, QT * c + QT)
                dve.wait_ge(std2_done, c + 1)
                chain(nc.vector.reciprocal(rstd2[:, tiles], std2[:, tiles]))
                nc.vector.scalar_tensor_tensor(out=shift2[:, tiles], in0=mean_var2[:, tiles, 0], scalar=-1.0,
                                               in1=rstd2[:, tiles], op0=ALU.mult, op1=ALU.mult).then_inc(rstd2_done, 1)

            def normalise_last():
                tiles = slice(QT * EARLY, TILES)
                dve.wait_ge(std2_done, EARLY + 1)
                chain(nc.vector.reciprocal(rstd2[:, tiles], std2[:, tiles]))
                for t in range(QT * EARLY, TILES):
                    last = nc.vector.tensor_scalar(rows[:, t, 0:D], rows[:, t, D:2 * D], mean_var2[:, t, 0:1],
                                                   rstd2[:, t:t + 1], ALU.subtract, ALU.mult)
                last.then_inc(last_xn2_done, 1)
                dve.wait_ge(last_xn2T_done, 1)
                nc.vector.tensor_copy(xn2T[:, QUARTER * EARLY:TOKENS], turn2_banks[EARLY % 2][:, :]
                                      ).then_inc(last_xn2T_copied, 1)

            last = UNITS - 1
            early = slice(0, Q * EARLY)
            mask_scores(last - 1, 0)
            rotate_qk(last, 1)
            mask_scores(last - 1, 1)
            add_heads(last - 1, 0)
            mask_scores(last, 0)
            add_heads(last - 1, 1)
            dve.wait_ge(head_zeroed, 2)
            invert_heads(0, early).then_inc(hrstd_done, 1)
            mask_scores(last, 1)
            add_heads(last, 0)
            close_attention(0)
            add_heads(last, 1)
            close_attention(1)
            statistics2(0)
            close_attention(2)
            invert_heads(1, slice(Q * EARLY, P)).then_inc(hrstd_done, 1)
            invert_std2(0)
            statistics2(1)
            close_attention(3)
            invert_std2(1)
            statistics2(2)
            statistics2(EARLY)
            invert_std2(2)
            normalise_last()
            dve.wait_ge(late_consts_in, 16)

            dve.wait_ge(bias_in, 64)
            dve.wait_ge(logitsT_done, 1)
            nc.vector.tensor_scalar(logitsT[:, 2 * P:4 * P], logit_banks[1][:, 0:2 * P], router_bias[:, 0:1], None, ALU.add
                                    ).then_inc(logitsT_copied, 1)
            dve.wait_ge(logits_turned, 1)

            def by_quarter(a):
                return a[:, :, :].rearrange("p (c k) e -> p c k e", c=4)

            logits = bank_gv[:, :].rearrange("p (k c e) -> p c k e", k=QT, c=4)[:, :, :, 0:EXPERTS]
            chain(nc.vector.tensor_reduce(top[:, :].rearrange("p (c k) -> p c k", c=4), logits, AX.X, ALU.max))
            top_b = top[:, :].rearrange("p (c k) -> p c k", c=4).unsqueeze(3).broadcast_to([P, 4, QT, EXPERTS])
            nc.vector.tensor_tensor(by_quarter(below_top), logits, top_b, ALU.subtract).then_inc(below_done, 1)
            dve.wait_ge(below_done, 1)
            chain(nc.vector.scalar_tensor_tensor(
                out=rank_of_top[:, :, :], in0=below_top[:, :, :], scalar=0.0,
                in1=const("expert_rank").unsqueeze(1).broadcast_to(te), op0=ALU.is_equal, op1=ALU.mult))
            chain(nc.vector.tensor_reduce(best_rank[:, :], rank_of_top[:, :, :], AX.X, ALU.max))
            nc.vector.tensor_tensor(chosen[:, :, :], rank_of_top[:, :, :],
                                    best_rank[:, :].unsqueeze(2).broadcast_to(te), ALU.is_equal).then_inc(chosen_done, 1)
            dve.wait_ge(powers_done, 1)
            chain(nc.vector.tensor_reduce(power_sum[:, :], powers[:, :, :], AX.X, ALU.add))
            nc.vector.reciprocal(top_weight[:, :], power_sum[:, :]).then_inc(weight_done, 1)

            dve.wait_ge(chosen_done, 1)
            dve.wait_ge(ranks_done, 1)
            et = [P, EXPERTS, TILES]
            ranks = bank_q[:, 0:P].rearrange("p (t e) -> p t e", e=EXPERTS)
            counts = bank_k[:, 0:P]
            chain(nc.vector.tensor_tensor_scan(counts_to[:, :, :].rearrange("p e t -> p (e t)"),
                                               const("not_first_tile"), counts, 0.0, ALU.mult, ALU.add))
            used = step(nc.vector.tensor_tensor(tiles_used[:, :, :], counts_to[:, :, TILES - 1:TILES].broadcast_to(et),
                                                const("tile_edge").unsqueeze(1).broadcast_to(et), ALU.is_gt))
            before = step(nc.vector.tensor_tensor(counts_before[:, :, :], counts_to[:, :, :],
                                                  counts.rearrange("p (e t) -> p e t", e=EXPERTS), ALU.subtract))
            dve.wait_ge(dve_step, used)
            tiles_of = step(nc.vector.tensor_reduce(n_tiles[:, :], tiles_used[:, :, :], AX.X, ALU.add))
            dve.wait_ge(dve_step, before)
            placed = step(nc.vector.tensor_tensor(place[:, :, :], ranks,
                                                  counts_before[:, :, :].rearrange("p e t -> p t e"), ALU.add))
            dve.wait_ge(dve_step, tiles_of)
            ends = step(nc.vector.tensor_tensor_scan(end_tile[:, :], const("ones")[:, 0:EXPERTS], n_tiles[:, :],
                                                     0.0, ALU.mult, ALU.add))
            dve.wait_ge(dve_step, placed)
            own_place = step(nc.vector.tensor_tensor(place_chosen[:, :, :], place[:, :, :], chosen[:, :, :], ALU.mult))
            dve.wait_ge(dve_step, ends)
            based = step(nc.vector.tensor_tensor(base[:, :], end_tile[:, :], n_tiles[:, :], ALU.subtract))
            dve.wait_ge(dve_step, own_place)
            ranked = step(nc.vector.tensor_reduce(rank[:, :], place_chosen[:, :, :], AX.X, ALU.add))
            dve.wait_ge(dve_step, based)
            own_base = step(nc.vector.tensor_tensor(base_chosen[:, :, :], base[:, :].unsqueeze(1).broadcast_to(te),
                                                    chosen[:, :, :], ALU.mult))
            dve.wait_ge(dve_step, ranked)
            whole = step(nc.vector.tensor_copy(rank_i[:, :], rank[:, :]))
            dve.wait_ge(dve_step, own_base)
            step(nc.vector.tensor_reduce(first_tile[:, :], base_chosen[:, :, :], AX.X, ALU.add))
            dve.wait_ge(dve_step, whole)
            step(nc.vector.tensor_scalar(rank_parts[:, 0, :], rank_i[:, :], 7, None, ALU.logical_shift_right))
            chain(nc.vector.tensor_scalar(rank_parts[:, 1, :], rank_i[:, :], P - 1, None, ALU.bitwise_and))
            nc.vector.tensor_tensor(slot_parts[:, 0, :], rank_parts[:, 0, :], first_tile[:, :], ALU.add)
            nc.vector.tensor_copy(slot_parts[:, 1, :], rank_parts[:, 1, :]).then_inc(slots_done, 1)
            dve.wait_ge(slots_done, 1)
            dve.wait_ge(converted, 3)
            ts = [P, TILES, SLOT_TILES]
            nc.vector.tensor_tensor(is_tile[:, :, :], slot_parts[:, 0, :].unsqueeze(2).broadcast_to(ts),
                                    iota_h[:, 0:SLOT_TILES].unsqueeze(1).broadcast_to(ts), ALU.is_equal
                                    ).then_inc(is_tile_done, 1)
            tl = [P, TILES, P]
            nc.vector.tensor_tensor(in_lane[:, :, :], iota_h[:, :].unsqueeze(1).broadcast_to(tl),
                                    slot_parts[:, 1, :].unsqueeze(2).broadcast_to(tl), ALU.is_equal).then_inc(lanes_done, 1)
            se = [P, SLOT_TILES, EXPERTS]
            chain(nc.vector.tensor_tensor(past_end[:, :, :],
                                          const("iota")[:, 0:SLOT_TILES].unsqueeze(2).broadcast_to(se),
                                          end_tile[:, :].unsqueeze(1).broadcast_to(se), ALU.is_ge))
            chain(nc.vector.tensor_reduce(tile_expert_f[:, :], past_end[:, :, :], AX.X, ALU.add))
            dve.wait_ge(inverse_done, 1)
            inverse = bank_o[0][:, 0:SLOT_TILES]
            nc.vector.tensor_scalar(indices[:, 0, :], inverse, 1.0, 0.0, ALU.subtract, ALU.max).then_inc(indices_done, 1)
            nc.vector.tensor_scalar(tile_expert[:, :], tile_expert_f[:, :], float(EXPERTS - 1), None, ALU.min
                                    ).then_inc(experts_known, 1)
            chain(nc.vector.tensor_scalar(no_token[:, :], inverse, 0.0, float(NO_TOKEN), ALU.is_equal, ALU.mult))
            nc.vector.scalar_tensor_tensor(out=indices[:, 1, :], in0=no_token[:, :], scalar=-1.0, in1=inverse,
                                           op0=ALU.add, op1=ALU.add).then_inc(targets_done, 1)

            dve.wait_ge(expert_w_in, 64)
            dve.wait_ge(experts_known, 1)

            def fetch_w1(i, r):
                e = dve.value_load(tile_expert[0:1, bass.ds(i, 1)], min_val=0, max_val=EXPERTS - 1)
                dve.wait_ge(hidden_done, START + i - 1)
                nc.vector.tensor_copy(w1_now[r][:, :], w1_all[:, bass.ds(e * HIDDEN, HIDDEN)]).then_inc(w1_copied, 1)

            def copy_slotT(i, r):
                dve.wait_ge(slotT_done, i + 1)
                dve.wait_ge(hidden_done, START + i - 1)
                nc.vector.tensor_copy(slotT[r][:, :], bank_s[r][:, 0:P]).then_inc(slotT_copied, 1)

            def finish(i, r, u):
                e = dve.value_load(tile_expert[0:1, bass.ds(i, 1)], min_val=0, max_val=EXPERTS - 1)
                dve.wait_ge(y_done, START + i + 1)
                nc.vector.tensor_tensor(y_bias[r][:, :], bank_o[r][:, 0:D], b2_all[:, bass.ds(e * D, D)], ALU.add
                                        ).then_inc(y_biased, 1)
                dve.wait_ge(y_biased, START + i + 1)
                nc.vector.scalar_tensor_tensor(out=got_rows[u][:, 0:D], in0=y_bias[r][:, :],
                                               scalar=got_rows[u][:, 2 * D:ROW], in1=got_rows[u][:, D:2 * D],
                                               op0=ALU.mult, op1=ALU.add).then_inc(out_done, 1)

            for i in range(2):
                fetch_w1(i, i)
            for i in range(2):
                copy_slotT(i, i)
            for i in range(SLOT_TILES):
                if i + 2 < SLOT_TILES:
                    copy_slotT(i + 2, i % 2)
                    fetch_w1(i + 2, i % 2)
                finish(i, i % 2, i % RING)

        @block.tensor
        def _(pe):
            mm = nc.tensor.matmul
            ident = const("ident")

            def keep_warm(n):
                for _ in range(n):
                    mm(bank_q[:, :], warm[:, 0:P], warm[:, :], start=True, stop=True)

            pe.wait_ge(warm_zeroed, 1)
            keep_warm(11)
            pe.wait_ge(consts_in, 16)
            pe.wait_ge(attn_w_in, 16)
            mm(bank_gv[:, 0:P], wat[:, 4, :], const("centre"), start=True, stop=True).then_inc(wv_done, 1)

            def turn(m, r, round_):
                pe.wait_ge(xn_done, m + 1)
                pe.wait_ge(ctx_ld[r], 16 * (round_ + 1))
                pe.wait_ge(xcT_done, m)
                for s, src in enumerate((xn[r], ctx_in[r])):
                    for j in range(2):
                        at = s * UNIT + j * P
                        last = nc.tensor.transpose(bank_t[:, at:at + P], src[:, j, :], ident)
                last.then_inc(xT_done, 1)

            def project_qk(m, r):
                pe.wait_ge(xcT_done, m + 1)
                for bank, w, src, free, done in ((bank_q, 0, 0, q_rotated, q_done), (bank_k, 2, UNIT, k_rotated, k_done)):
                    pe.wait_ge(free, m)
                    for s in range(2):
                        last = mm(bank[:, s * UNIT:s * UNIT + UNIT], wat[:, w + s, :], xcT[r][:, src:src + UNIT],
                                  start=True, stop=True)
                    last.then_inc(done, 1)

            def project_gv(m, r):
                pe.wait_ge(gv_copied, m)
                mm(bank_gv[:, 0:UNIT], wat[:, 5, :], xcT[r][:, 0:UNIT], start=True, stop=True)
                for j in range(2):
                    last = mm(bank_gv[:, UNIT + P * j:UNIT + P * j + P],
                              xcT[r][:, UNIT + P * j:UNIT + P * j + P], w_v[:, :], start=True, stop=True)
                last.then_inc(gv_done, 1)

            def scores(m, r, j):
                if j == 0:
                    pe.wait_ge(qh_done, START + m + 1)
                    pe.wait_ge(last_qh_done, START + m + 1)
                    pe.wait_ge(kh_done, START + m + 1)
                for half in range(2):
                    pe.wait_ge(sim_done, START + 4 * m + 2 * j + half - 1)
                    for block in range(2):
                        for b in range(2):
                            at = HK * (2 * (block ^ half) + b)
                            keys = j * P + HK * (2 * block + b)
                            first = HK * block
                            last = mm(bank_s[half][at:at + HK, :].rearrange("p (h i) -> p h i", i=SEQ)[:, :, first:SEQ],
                                      k_halves[r][:, half, keys:keys + HK],
                                      q_heads[r][:, 2 * j + b, :, first:SEQ], start=True, stop=True)
                    last.then_inc(scores_done, 1)

            def products(m, r, j):
                tile = 2 * m + j
                if j == 0:
                    pe.wait_ge(gv_copied, m + 1)
                pe.wait_ge(sim_done, START + 4 * m + 2 * j + 2)
                pe.wait_ge(ret_done, START + tile - 1)
                for b in range(2):
                    for g in range(GROUPS):
                        last = mm(bank_o[j][Q * g:Q * g + Q, 256 * b:256 * b + 256],
                                  v_batches[r][:, j, b, Q * g:Q * g + Q],
                                  sim[j][:, g // 2, 256 * (g % 2):256 * (g % 2) + 256], start=True, stop=True)
                last.then_inc(av_done, 1)

            def unit(m, r, round_):
                scores(m, r, 0)
                project_qk(m + 1, 1 - r)
                products(m, r, 0)
                scores(m, r, 1)
                project_gv(m + 1, 1 - r)
                turn(m + 2, r, round_ + 1)
                products(m, r, 1)

            turn(0, 0, 0)
            project_qk(0, 0)
            pe.wait_ge(wv_copied, 1)
            project_gv(0, 0)
            turn(1, 1, 0)
            pe.wait_ge(sim_zeroed, 4)
            pe.wait_ge(first_qh_done, 1)
            with pe.Fori(0, (UNITS - 2) // 2) as n:
                for r in range(2):
                    unit(2 * n + r, r, n)

            def variances(k, bank, quarters):
                for c in quarters:
                    pe.wait_ge(squared, c + 1)
                    for h in range(2):
                        at = QUARTER * c + UNIT * h
                        last = mm(bank[Q * c:Q * c + Q, 0:UNIT], const("head_mean", 2)[:, h, :], squares[:, at:at + UNIT],
                                  start=(h == 0), stop=(h == 1))
                last.then_inc(hvar_done, 1)

            def spread(c):
                pe.wait_ge(hrstd_done, 1 + c // EARLY)
                if c >= 2:
                    pe.wait_ge(attn_done, c - 1)
                for h in range(2):
                    last = mm((bank_q, bank_k)[c % 2][:, UNIT * h:UNIT * h + UNIT], const("spread", UNITS)[:, 2 * c + h, :],
                              head_rstd[c // EARLY][:, :], start=True, stop=True)
                last.then_inc(spread_done, 1)

            def start_x1(c):
                pe.wait_ge(xb_done, c + 1)
                if c >= 2:
                    pe.wait_ge(x1_done, c - 1)
                mm(proj_banks[c % 2][:, :], ident, x_plus_b[:, QT * c:QT * c + QT, :].rearrange("p t d -> p (t d)"),
                   start=True, stop=False)

            def project_out(c):
                pe.wait_ge(attn_done, c + 1)
                for t in range(QT):
                    last = mm(proj_banks[c % 2][:, P * t:P * t + P], attn[c % 2][:, P * t:P * t + P], wat[:, 6, :],
                              start=False, stop=(t == QT - 1))
                last.then_inc(proj_done, 1)

            def turn_xn2(c):
                if c < EARLY:
                    pe.wait_ge(xn2_done, c + 1)
                else:
                    pe.wait_ge(last_xn2_done, 1)
                if c >= 2:
                    pe.wait_ge(xn2T_copied, c - 1)
                for t in range(QT):
                    last = nc.tensor.transpose(turn2_banks[c % 2][:, P * t:P * t + P], rows[:, QT * c + t, 0:D], ident)
                last.then_inc(xn2T_done if c < EARLY else last_xn2T_done, 1)

            def route(c):
                if c < EARLY:
                    pe.wait_ge(xn2T_copied, c + 1)
                else:
                    pe.wait_ge(last_xn2T_copied, 1)
                pe.wait_ge(hstd_done, 2)
                for h, bank in enumerate(logit_banks):
                    at = QUARTER * c + 2 * P * h
                    last = mm(bank[Q * c:Q * c + Q, 0:2 * P], router_w[:, :], xn2T[:, at:at + 2 * P], start=True, stop=True)
                return last

            pe.wait_ge(late_consts_in, 16)
            pe.wait_ge(bias_in, 64)
            last = UNITS - 1
            scores(last - 1, 0, 0)
            project_qk(last, 1)
            variances(0, bank_t, range(EARLY))
            products(last - 1, 0, 0)
            scores(last - 1, 0, 1)
            project_gv(last, 1)
            products(last - 1, 0, 1)
            scores(last, 1, 0)
            products(last, 1, 0)
            pe.wait_ge(gv_copied, UNITS)
            start_x1(0)
            scores(last, 1, 1)
            spread(0)
            spread(1)
            products(last, 1, 1)
            project_out(0)
            start_x1(1)
            spread(2)
            variances(1, bank_t, range(EARLY, 4))
            project_out(1)
            start_x1(2)
            project_out(2)
            spread(3)
            start_x1(3)
            project_out(3)
            turn_xn2(0)
            keep_warm(4)
            turn_xn2(1)
            route(0)
            route(1)
            turn_xn2(3)
            turn_xn2(2)
            route(2)
            route(3).then_inc(logitsT_done, 1)
            pe.wait_ge(logitsT_copied, 2)
            for k in range(QT):
                last = nc.tensor.transpose(bank_gv[:, P * k:P * k + P], logitsT[:, P * k:P * k + P], ident)
            last.then_inc(logits_turned, 1)
            pe.wait_ge(chosen_done, 1)
            chosen_cols = chosen[:, :, :].rearrange("p t e -> p (t e)")
            pe.wait_ge(converted, 3)
            mm(bank_q[:, 0:P], before_ones[:, 0, :], chosen_cols, start=True, stop=True)
            mm(bank_k[:, 0:P].rearrange("p (e t) -> p e t", e=EXPERTS), before_ones[:, 1, :],
               chosen[:, :, :].rearrange("p t e -> p e t"), start=True, stop=True).then_inc(ranks_done, 1)
            pe.wait_ge(slots_done, 1)
            keep_warm(6)
            pe.wait_ge(in_tile_done, 1)
            pe.wait_ge(lanes_done, 1)
            for t in range(TILES):
                last = mm(bank_o[0][:, 0:SLOT_TILES], in_lane[:, t, :], in_tile[:, t, :],
                          start=(t == 0), stop=(t == TILES - 1))
            last.then_inc(inverse_done, 1)
            keep_warm(12)

            pe.wait_ge(expert_w_in, 64)
            pe.wait_ge(experts_known, 1)

            def turn_rows(i, r, u, round_):
                pe.wait_ge(got[u], 16 * (round_ + 1))
                pe.wait_ge(slotT_copied, START + i - 1)
                nc.tensor.transpose(bank_s[r][:, 0:P], got_rows[u][:, 0:D], ident).then_inc(slotT_done, 1)

            def first_layer(i, r):
                pe.wait_ge(slotT_copied, START + i + 1)
                pe.wait_ge(w1_copied, i + 1)
                pe.wait_ge(silu_done, START + i - 1)
                for c in range(HC):
                    last = mm((bank_q, bank_k)[r][:, P * c:P * c + P], w1_now[r][:, P * c:P * c + P], slotT[r][:, :],
                              start=True, stop=True)
                last.then_inc(hidden_done, 1)

            def second_layer(i, r):
                e = pe.value_load(tile_expert[0:1, bass.ds(i, 1)], min_val=0, max_val=EXPERTS - 1)
                pe.wait_ge(silu_done, START + i + 1)
                pe.wait_ge(y_biased, START + i - 1)
                for c in range(HC):
                    last = mm(bank_o[r][:, 0:D], hiddenT[r][:, c, :], w2_all[:, bass.ds((e * HC + c) * D, D)],
                              start=(c == 0), stop=(c == HC - 1))
                last.then_inc(y_done, 1)

            turn_rows(0, 0, 0, 0)
            first_layer(0, 0)
            turn_rows(1, 1, 1, 0)
            for i in range(SLOT_TILES):
                if i + 2 < SLOT_TILES:
                    turn_rows(i + 2, i % 2, (i + 2) % RING, (i + 2) // RING)
                if i + 1 < SLOT_TILES:
                    first_layer(i + 1, 1 - i % 2)
                second_layer(i, i % 2)


def constants():
    f = np.float32
    p = np.arange(P)
    head, dim = p // HD, p % HD
    pos = np.arange(SEQ)
    even = np.arange(0, HD, 2, dtype=f)
    length_base = ((even + f(0.4 * HD)) / f(1.4 * HD)).astype(f)
    power = (np.arange(-(SEQ // 2), SEQ - SEQ // 2, dtype=f) / f(512.0))[:, None]
    scale = length_base.astype(np.float64)[None, :] ** power.astype(np.float64)
    half = HD // 2
    inv_freq = (1.0 / 10000.0 ** (np.arange(half, dtype=np.float64) / half)).astype(f)
    angle = (pos.astype(f)[:, None] * inv_freq[None, :]).astype(np.float64)
    sin, cos = np.sin(angle), np.cos(angle)
    gamma = 1.0 - np.exp(np.linspace(np.log(1.0 / 32.0), np.log(1.0 / 512.0), HEADS)).astype(f)
    gamma = gamma.astype(f).astype(np.float64)[head][:, None]
    sign = np.where(dim % 2 == 0, -1.0, 1.0)[:, None]
    pair = dim // 2
    up, down = gamma ** pos[None, :], gamma ** -pos[None, :].astype(np.float64)
    q_tables = [(cos * scale).T[pair] * up, (sin * scale).T[pair] * up * sign]
    k_tables = [(cos / scale).T[pair] * down, (sin / scale).T[pair] * down * sign]
    key = HK * (p // (2 * HK)) + p % HK
    quad, lane = p // Q, p % Q
    mean_of_head = np.where(head[:, None] == np.arange(HEADS)[None, :], 1.0 / HD, 0.0)
    nothing = np.zeros((P, HEADS))
    head_mean = np.concatenate([mean_of_head, nothing, nothing, mean_of_head], axis=1)
    spread = np.concatenate([((quad == m // 2) & (lane // HEADS == m % 2))[:, None] *
                             ((lane % HEADS)[:, None] == head[None, :]) for m in range(UNITS)], axis=1)
    full = {
        "ident": np.eye(P),
        "rotary_q": np.concatenate(q_tables, axis=1),
        "rotary_k": np.concatenate([t[:, key] for t in k_tables], axis=1),
        "causal": np.concatenate([key[:, None] <= pos[None, :], np.roll(key, P // 2)[:, None] <= pos[None, :]], axis=1),
        "head_in_half": (head % HH)[:, None] == np.arange(HH)[None, :],
        "batch_of_key": (p // HK % 2)[:, None] == np.arange(2)[None, :],
        "head_in_group": (head % GH)[:, None] == np.arange(GH)[None, :],
        "eps": np.full((P, 1), EPS),
        "centre": np.eye(P) - (head[:, None] == head[None, :]) / HD,
        "head_mean": head_mean,
        "spread": spread,
        "before": p[:, None] < p[None, :],
        "ones": np.ones((P, P)),
        "iota": np.tile(p, (P, 1)),
        "token_number": P * np.arange(TILES)[None, :] + p[:, None] + 1,
        "expert_rank": np.tile(EXPERTS - np.arange(EXPERTS), (P, 1)),
        "tile_edge": np.tile(P * np.arange(TILES), (P, 1)),
        "not_first_tile": np.tile(np.arange(EXPERTS * TILES) % TILES != 0, (P, 1)),
    }
    out = np.zeros((P, CONST_WIDTH), f)
    for name, _ in CONST_PARTS:
        at, width = CONST_AT[name]
        out[:, at:at + width] = full[name]
    return out


def kernel(x, ctx_1024, L0_xattn_W_Q, L0_xattn_W_K, L0_xattn_W_V, L0_xattn_g_w, L0_xattn_g_b, L0_xattn_out_w,
           L0_xattn_out_b, L0_ffn_Wg, L0_ffn_bg, L0_ffn_W1, L0_ffn_b1, L0_ffn_W2, L0_ffn_b2):
    import concourse.bacc as bacc
    from concourse.bass_utils import run_bass_kernel_spmd

    def per_head(w):
        return np.asarray(w).transpose(1, 0, 2).reshape(D, D)

    swap = np.arange(D) ^ 1
    w_q, w_k, w_v = per_head(L0_xattn_W_Q), per_head(L0_xattn_W_K), per_head(L0_xattn_W_V)
    stacked = [w_q, w_q[:, swap], w_k, w_k[:, swap], w_v.T, np.asarray(L0_xattn_g_w).T, np.asarray(L0_xattn_out_w).T]
    router = np.zeros((D, Q), np.float32)
    router[:, :EXPERTS] = np.asarray(L0_ffn_Wg)
    router_bias = np.zeros((4, Q), np.float32)
    router_bias[:, :EXPERTS] = np.asarray(L0_ffn_bg)
    arrays = {
        "x": np.asarray(x).reshape(TOKENS, D),
        "ctx": np.asarray(ctx_1024).reshape(TILES, 2, 2, HK, D).transpose(0, 2, 1, 3, 4).reshape(TOKENS, D),
        "w_attn": np.stack(stacked, axis=1),
        "g_b": np.asarray(L0_xattn_g_b).reshape(D, 1),
        "out_b": np.asarray(L0_xattn_out_b),
        "w_gate": router,
        "b_gate": router_bias.reshape(P, 1),
        "w1": np.asarray(L0_ffn_W1).transpose(1, 0, 2).reshape(D, EXPERTS * HIDDEN),
        "b1": np.asarray(L0_ffn_b1).reshape(EXPERTS * HC, P).T,
        "w2": np.asarray(L0_ffn_W2).reshape(EXPERTS, HC, P, D).transpose(2, 0, 1, 3).reshape(P, EXPERTS * HC * D),
        "b2": np.asarray(L0_ffn_b2).reshape(EXPERTS * D),
        "consts": constants(),
    }
    nc = bacc.Bacc("TRN2", target_bir_lowering=False, num_devices=1)
    args, ins = [], {}
    for name, a in arrays.items():
        ins[f"in_{name}"] = np.ascontiguousarray(a)
        args.append(nc.dram_tensor(f"in_{name}", a.shape, mybir.dt.from_np(a.dtype), kind="ExternalInput").ap())
    out = nc.dram_tensor("out", (TOKENS, D), F32, kind="ExternalOutput").ap()
    build(nc, *args, out)
    result = run_bass_kernel_spmd(nc, [ins], core_ids=[0])
    return result.results[0]["out"].reshape(BATCH, SEQ, D)
```
